# Optimizing a Trainium2 kernel written in Bass

```python
import numpy as np
import jax
import jax.numpy as jnp

def _softmax(x, axis=-1):
    return jax.nn.softmax(x, axis=axis)

def _gelu(x):
    return jax.nn.gelu(x, approximate=True)

def _silu(x):
    return jax.nn.silu(x)

def _sigmoid(x):
    return jax.nn.sigmoid(x)

def _layernorm(x, axis=-1, eps=1e-05):
    m = jnp.mean(x, axis=axis, keepdims=True)
    v = jnp.var(x, axis=axis, keepdims=True)
    return (x - m) / jnp.sqrt(v + eps)

def _scatter_add(tgt, idx, src, axis=0):
    return tgt.at[idx].add(src)

def _segment_sum(src, seg, n):
    return jax.ops.segment_sum(src, seg, n)
kernel_name = 'mk_recurrent_d1_jaxref_r8_319757'

def setup_inputs(seed: int=0):
    np.random.seed(seed)
    _w = jnp.asarray

    def _L0_attn_setup():
        import jax, jax.numpy as jnp
        import numpy as np
        D_MODEL = 128
        N_SCALES = 2
        R_MIN, R_MAX = (0.9, 0.999)
        TH_MIN, TH_MAX = (0.01, 1.0)
        B, S, D_IN = (4, 512, 128)
        D_PER = D_MODEL // N_SCALES

        def _scan_op(q_i, q_j):
            a_i, b_i = q_i
            a_j, b_j = q_j
            return (a_i * a_j, a_j * b_i + b_j)
        key = jax.random.key(seed)
        ks = jax.random.split(key, 16)
        scale = 1.0 / np.sqrt(D_IN)
        inp = {'x': jax.random.normal(ks[0], (B, S, D_IN), jnp.float32)}
        k = 1
        for i in range(N_SCALES):
            inp[f'W_re{i}'] = jax.random.normal(ks[k], (D_IN, D_PER), jnp.float32) * scale
            k += 1
            inp[f'b_re{i}'] = jnp.zeros((D_PER,), jnp.float32)
            inp[f'W_im{i}'] = jax.random.normal(ks[k], (D_IN, D_PER), jnp.float32) * scale
            k += 1
            inp[f'b_im{i}'] = jnp.zeros((D_PER,), jnp.float32)
        inp['W_gate'] = jax.random.normal(ks[k], (D_MODEL, D_MODEL), jnp.float32) * (1.0 / np.sqrt(D_MODEL))
        inp['b_gate'] = jnp.zeros((D_MODEL,), jnp.float32)
        return inp
    _L0_attn_in = _L0_attn_setup()

    def _L0_ffn_setup():
        import jax, jax.numpy as jnp
        import numpy as np
        B, T, D = (1, 128, 128)
        E, S, H = (8, 2, 512)
        key = jax.random.key(seed)
        kx, kg, k1, k2, k3 = jax.random.split(key, 5)
        X = jax.random.normal(kx, (B, T, D), jnp.float32)
        Wg = jax.random.normal(kg, (D, E), jnp.float32) * 0.02
        bg = jnp.zeros((E,), jnp.float32)
        W1 = jax.random.normal(k1, (E, D, H), jnp.float32) * 0.02
        W3 = jax.random.normal(k3, (E, D, H), jnp.float32) * 0.02
        W2 = jax.random.normal(k2, (E, H, D), jnp.float32) * 0.02
        return {'X': X, 'Wg': Wg, 'bg': bg, 'W1': W1, 'W2': W2, 'W3': W3}
    _L0_ffn_in = _L0_ffn_setup()
    _d = {'L0_attn_x': _L0_attn_in['x'], 'L0_attn_W_re0': _L0_attn_in['W_re0'], 'L0_attn_b_re0': _L0_attn_in['b_re0'], 'L0_attn_W_im0': _L0_attn_in['W_im0'], 'L0_attn_b_im0': _L0_attn_in['b_im0'], 'L0_attn_W_re1': _L0_attn_in['W_re1'], 'L0_attn_b_re1': _L0_attn_in['b_re1'], 'L0_attn_W_im1': _L0_attn_in['W_im1'], 'L0_attn_b_im1': _L0_attn_in['b_im1'], 'L0_attn_W_gate': _L0_attn_in['W_gate'], 'L0_attn_b_gate': _L0_attn_in['b_gate'], 'L0_ffn_Wg': _L0_ffn_in['Wg'], 'L0_ffn_bg': _L0_ffn_in['bg'], 'L0_ffn_W1': _L0_ffn_in['W1'], 'L0_ffn_W2': _L0_ffn_in['W2'], 'L0_ffn_W3': _L0_ffn_in['W3']}
    _x0 = _d['L0_attn_x']
    _d['L0_attn_x'] = jax.random.normal(jax.random.fold_in(jax.random.key(seed), 1), (16, 256, 128), dtype=_x0.dtype)
    del _x0
    return _d

def reference(L0_attn_x, L0_attn_W_re0, L0_attn_b_re0, L0_attn_W_im0, L0_attn_b_im0, L0_attn_W_re1, L0_attn_b_re1, L0_attn_W_im1, L0_attn_b_im1, L0_attn_W_gate, L0_attn_b_gate, L0_ffn_Wg, L0_ffn_bg, L0_ffn_W1, L0_ffn_W2, L0_ffn_W3):

    def _L0_attn_ref(x, W_re0, b_re0, W_im0, b_im0, W_re1, b_re1, W_im1, b_im1, W_gate, b_gate):
        import jax, jax.numpy as jnp
        import numpy as np
        D_MODEL = 128
        N_SCALES = 2
        R_MIN, R_MAX = (0.9, 0.999)
        TH_MIN, TH_MAX = (0.01, 1.0)
        B, S, D_IN = (4, 512, 128)
        D_PER = D_MODEL // N_SCALES

        def _scan_op(q_i, q_j):
            a_i, b_i = q_i
            a_j, b_j = q_j
            return (a_i * a_j, a_j * b_i + b_j)
        r_vals = np.linspace(R_MAX, R_MIN, N_SCALES)
        th_vals = np.linspace(TH_MIN, TH_MAX, N_SCALES)
        Ws = [(W_re0, b_re0, W_im0, b_im0), (W_re1, b_re1, W_im1, b_im1)]
        h_scales = []
        for i in range(N_SCALES):
            r = float(r_vals[i])
            theta = float(th_vals[i])
            a_c = np.complex64(r * np.exp(1j * theta))
            W_re, b_re, W_im, b_im = Ws[i]
            b = (x @ W_re + b_re + 1j * (x @ W_im + b_im)).astype(jnp.complex64) * (1.0 - r)
            a = jnp.full(b.shape, a_c, dtype=jnp.complex64)
            _, h = jax.lax.associative_scan(_scan_op, (a, b), axis=1)
            h_scales.append(h.real)
        h = jnp.concatenate(h_scales, axis=-1)
        gate = jax.nn.sigmoid(h @ W_gate + b_gate)
        return gate * h

    def _L0_ffn_ref(X, Wg, bg, W1, W2, W3):
        import jax, jax.numpy as jnp
        import numpy as np
        B, T, D = (1, 128, 128)
        E, S, H = (8, 2, 512)
        logits = jnp.einsum('btd,de->bte', X, Wg) + bg
        topv, topi = jax.lax.top_k(logits, S)
        w = jax.nn.softmax(topv, axis=-1)
        xs = X[:, :, None, :] * w[..., None]
        out = X
        for e in range(E):
            h = jax.nn.silu(jnp.einsum('btsd,dh->btsh', xs, W1[e])) * jnp.einsum('btsd,dh->btsh', xs, W3[e])
            y = jnp.einsum('btsh,hd->btsd', h, W2[e])
            mask = (topi == e)[..., None]
            out = out + jnp.where(mask, y, 0.0).sum(axis=2)
        return out
    x = L0_attn_x
    xn = _layernorm(x, axis=-1)
    s = _L0_attn_ref(xn, L0_attn_W_re0, L0_attn_b_re0, L0_attn_W_im0, L0_attn_b_im0, L0_attn_W_re1, L0_attn_b_re1, L0_attn_W_im1, L0_attn_b_im1, L0_attn_W_gate, L0_attn_b_gate)
    g = _silu(_L0_ffn_ref(xn, L0_ffn_Wg, L0_ffn_bg, L0_ffn_W1, L0_ffn_W2, L0_ffn_W3))
    x = x + s * g
    return x

_drawn_inputs = setup_inputs


def setup_inputs(seed=0):
    import zlib

    import numpy as np

    out = dict(_drawn_inputs(seed))
    spreads = {'L0_attn_b_re0': (0.0, 0.8),
     'L0_attn_b_im0': (0.0, 0.8),
     'L0_attn_b_re1': (0.0, 0.8),
     'L0_attn_b_im1': (0.0, 0.8),
     'L0_attn_b_gate': (0.0, 0.8),
     'L0_ffn_bg': (0.0, 0.8)}
    factors = {'L0_attn_W_re0': 8.0,
     'L0_attn_W_im0': 8.0,
     'L0_attn_W_gate': 8.0,
     'L0_ffn_Wg': 8.0,
     'L0_ffn_W1': 8.0,
     'L0_ffn_W2': 8.0,
     'L0_ffn_W3': 8.0}
    for name, (base, spread) in spreads.items():
        noise = np.random.default_rng([zlib.crc32(name.encode()), seed]).standard_normal(out[name].shape)
        drawn = base * np.exp(spread * noise) if base else spread * noise
        out[name] = jnp.asarray(drawn.astype(out[name].dtype))
    for name, factor in factors.items():
        out[name] = (out[name] * factor).astype(out[name].dtype)
    return out
```

```python
from contextlib import ExitStack

import numpy as np

import concourse.bass as bass
import concourse.mybir as mybir

F32 = mybir.dt.float32
F32R = mybir.dt.float32r
BF16 = mybir.dt.bfloat16
I32 = mybir.dt.int32
U32 = mybir.dt.uint32
ALU = mybir.AluOpType
ACT = mybir.ActivationFunctionType
X = mybir.AxisListType.X

P = 128
B, S, D = 16, 256, 128
TOK = B * S
NT = TOK // P
E, K, HID = 8, 2, 512
NC = HID // P
SC = 2
DP = D // SC
UW = 2 * SC * DP
GT = 8
NG = NT // GT
GB = GT // 2
HT4 = GT // 2
ROW = D + 1
REG = TOK + P
IDLE = E * REG
J = K * TOK // P + E
RING = 4
EW = 3 * HID
DUMP = K * TOK
EPS = 1e-5
LOWEST = -3.0e38
R_VALS = np.linspace(0.999, 0.9, SC)
TH_VALS = np.linspace(0.01, 1.0, SC)


def mixing_tables():
    blocks = np.zeros((P, SC, 2, 2, P), np.float64)
    sums = np.zeros((2, SC, S), np.float64)
    lag = np.arange(P)[None, :] - np.arange(P)[:, None]
    for i in range(SC):
        a = complex(np.complex64(float(R_VALS[i]) * np.exp(1j * float(TH_VALS[i]))))
        powers = float(np.float32(1.0 - float(R_VALS[i]))) * np.exp(np.log(a) * np.arange(S))
        for part, f in enumerate((powers.real, -powers.imag)):
            blocks[:, i, part, 0] = np.where(lag >= 0, f[np.maximum(lag, 0)], 0.0)
            blocks[:, i, part, 1] = f[lag + P]
            sums[part, i] = np.cumsum(f)
    return blocks.reshape(P, -1).astype(np.float32), sums.reshape(2, -1).astype(np.float32)


def build(nc, x, w_re0, b_re0, w_im0, b_im0, w_re1, b_re1, w_im1, b_im1, w_gate, b_gate,
          w_g, b_g, w1, w2, w3, mix, mix_sums, out):
    rows_dram = nc.dram_tensor("rows_dram", (IDLE + P, ROW), F32).ap()
    y_dram = nc.dram_tensor("y_dram", (K * TOK, D), F32).ap()
    xn_dram = nc.dram_tensor("xn_dram", (TOK, D), F32).ap()

    x_tiles = x.rearrange("b (h p) d -> p (b h) d", p=P)
    out_tiles = out.rearrange("b (h p) d -> p (b h) d", p=P)
    xn_tiles = xn_dram.rearrange("(n p) d -> p n d", p=P)
    y_tiles = y_dram.rearrange("(s n p) d -> p s n d", p=P, s=K)

    ctx = ExitStack()
    with ctx:
        def keep(name, shape, dt):
            return ctx.enter_context(nc.sbuf_tensor(name, shape, dt))

        def sem(name):
            return ctx.enter_context(nc.semaphore(name))

        ident = keep("ident", [P, P], F32)
        ew_hi = keep("ew_hi", [P, E * EW], F32R)
        ew_lo = keep("ew_lo", [P, E * EW], F32R)
        gated = keep("gated", [P, NT, D], F32)
        plan = keep("plan", [1, 2 * J + E], I32)
        banks = [ctx.enter_context(nc.psum_tensor(f"bank{i}", [P, 512], F32)) for i in range(8)]

        dispatch(nc, sem, banks, ident, ew_hi, ew_lo, gated, plan, rows_dram, xn_tiles, x_tiles,
                 (w_re0, w_im0, w_re1, w_im1), (b_re0, b_im0, b_re1, b_im1), w_gate, b_gate,
                 w_g, b_g, w1, w2, w3, mix, mix_sums)
        x_all = keep("x_all", [P, NT, D], F32)
        xn_all = keep("xn_all", [P, NT, D], F32)
        tail_in = sem("tail_in")
        experts(nc, sem, banks, ident, ew_hi, ew_lo, plan, rows_dram, y_dram, x_tiles, xn_tiles,
                x_all, xn_all, tail_in)
        combine(nc, sem, gated, x_all, xn_all, tail_in, y_tiles, out_tiles)


def dispatch(nc, sem, banks, ident, ew_hi, ew_lo, gated, plan, rows_dram, xn_tiles, x_tiles,
             w_proj, b_proj, w_gate, b_gate, w_g, b_g, w1, w2, w3, mix, mix_sums):
    ctx = ExitStack()
    with ctx:
        def sb(name, shape, dt):
            return ctx.enter_context(nc.sbuf_tensor(name, shape, dt))

        PW = UW + E
        ones = sb("ones", [P, P], F32)
        ones_bf = sb("ones_bf", [P, P], BF16)
        ones_r = sb("ones_r", [1, P], F32R)
        before = sb("before", [P, P], BF16)
        first_key = sb("first_key", [P, E], F32)
        region = sb("region", [P, E], F32)
        keep_sum = sb("keep_sum", [P, E, GT + 1], F32)
        half_power = sb("half_power", [P, GT], F32)
        steps = sb("steps", [1, J], F32)
        dest = sb("dest", [P, K * GT], F32)
        pad_row = sb("pad_row", [P, ROW], F32)

        proj_hi = sb("proj_hi", [P, PW], F32R)
        proj_lo = sb("proj_lo", [P, PW], F32R)
        gate_hi = sb("gate_hi", [P, D], F32R)
        gate_lo = sb("gate_lo", [P, D], F32R)
        gbias_raw = sb("gbias_raw", [1, D], F32)
        gbias_hi = sb("gbias_hi", [1, D], F32R)
        gbias_lo = sb("gbias_lo", [1, D], F32R)
        mix_hi = sb("mix_hi", [P, SC * 4 * P], F32R)
        mix_lo = sb("mix_lo", [P, SC * 4 * P], F32R)
        h_bias = sb("h_bias", [P, 2, D], F32)
        g_bias = sb("g_bias", [P, E], F32)

        ew_raw = sb("ew_raw", [P, 2, EW], F32)
        mix_raw = ew_raw[:, 0, 0:SC * 4 * P]
        proj_raw, gate_raw = ew_raw[:, 1, 0:PW], ew_raw[:, 1, PW:PW + D]
        sums = ew_raw[0:2, 1, PW + D:PW + D + SC * S]
        pbias = ew_raw[0:2, 1, PW + D + SC * S:PW + 2 * D + SC * S]
        x_in_sb = sb("x_in_sb", [P, 2, GT, D], F32)
        xn = sb("xn", [P, 2, GT, D], F32)
        stats = sb("stats", [P, GT, 6], F32)
        moments = sb("moments", [P, GT, 2], F32)
        var_eps = sb("var_eps", [P, GT], F32)
        rstd = sb("rstd", [P, GT], F32)
        xt_hi = sb("xt_hi", [P, 2, HT4 * P], F32R)
        xt_lo = sb("xt_lo", [P, 2, HT4 * P], F32R)
        u_hi = sb("u_hi", [P, GT, UW], F32R)
        u_lo = sb("u_lo", [P, GT, UW], F32R)
        h = sb("h", [P, GT, D], F32)
        ht_hi, ht_lo = xt_hi, xt_lo
        rows = sb("rows", [P, 2, K * GT, ROW], F32)
        slot_row = sb("slot_row", [P, 2, K * GT], U32)

        logits = sb("logits", [P, GT, E], F32)
        logits2 = sb("logits2", [P, GT, E], F32)
        key = sb("key", [P, 2, GT, E], F32)
        chosen = sb("chosen", [P, K, GT, E], F32)
        best = sb("best", [P, K, GT], F32)
        best_key = sb("best_key", [P, K, GT], F32)
        gap = sb("gap", [P, GT], F32)
        ratio = sb("ratio", [P, GT], F32)
        denom = sb("denom", [P, GT], F32)
        weight = sb("weight", [P, K, GT], F32)
        mask = sb("mask", [P, E, GT + 1], BF16)
        prefix = sb("prefix", [P, E, GT + 1], BF16)
        position = sb("position", [P, E, GT], F32)
        picked = sb("picked", [P, K, GT, E], F32)

        count = sb("count", [1, E], F32)
        padded = sb("padded", [1, E], I32)
        tiles_i = sb("tiles_i", [1, E], I32)
        tiles_f = sb("tiles_f", [1, E], F32)
        tile_end = sb("tile_end", [1, E], F32)
        jump = sb("jump", [1, E], F32)
        passed, jumped = (ew_raw[0:1, j, 0:J * E].rearrange("p (j e) -> p j e", e=E) for j in range(2))
        plan_f = sb("plan_f", [1, 2, J], F32)
        plan_g = sb("plan_g", [1, J], F32)
        tail_f = sb("tail_f", [1, E], F32)

        xt_bank, u_bank, h_bank = banks[0:2], banks[2:4], banks[4:6]
        pos_bank, gate_bank = banks[6], banks[7]

        consts_in, mix_in = sem("consts_in"), sem("mix_in")
        filled, filled2, made = sem("filled"), sem("filled2"), sem("made")
        split_hi, split_lo = sem("split_hi"), sem("split_lo")
        mix_hi_done, mix_lo_done = sem("mix_hi_done"), sem("mix_lo_done")
        hb_ready, hb_done = sem("hb_ready"), sem("hb_done")
        gb_ready, gb_done = sem("gb_ready"), sem("gb_done")
        x_in = [sem(f"x_in{k}") for k in range(2)]
        w_in = [sem(f"w_in{k}") for k in range(2)]
        xn_out = [sem(f"xn_out{k}") for k in range(2)]
        rows_free = sem("rows_free")
        sent = [sem(f"sent{k}") for k in range(2)]
        stats_seen = sem("stats_seen")
        stats_done, moments_done, var_done = sem("stats_done"), sem("moments_done"), sem("var_done")
        rstd_done, xn_done = sem("rstd_done"), sem("xn_done")
        xt_ready, xt_hi_done, xt_lo_done = sem("xt_ready"), sem("xt_hi_done"), sem("xt_lo_done")
        xt_free = sem("xt_free")
        u_ready, u_hi_done, u_free = sem("u_ready"), sem("u_hi_done"), sem("u_free")
        logits_done = sem("logits_done")
        h_ready, h_free = sem("h_ready"), sem("h_free")
        ht_ready, ht_hi_done = sem("ht_ready"), sem("ht_hi_done")
        gate_ready, gate_free, tanh_done = sem("gate_ready"), sem("gate_free"), sem("tanh_done")
        route = sem("route")
        gap_done, exp_done, weight_done = sem("gap_done"), sem("exp_done"), sem("weight_done")
        prefix_done, pos_ready = sem("prefix_done"), sem("pos_ready")
        idx_done, dest_done = sem("idx_done"), sem("dest_done")
        row0_done, row1_done = sem("row0_done"), sem("row1_done")
        w_hi_done, w_lo_done = sem("w_hi_done"), sem("w_lo_done")
        count_ready, planning, planned = sem("count_ready"), sem("planning"), sem("planned")
        pad_out = sem("pad_out")

        block = ctx.enter_context(nc.Block())

        def groups(eng, body):
            with eng.Fori(0, NG // 2) as r:
                for k in range(2):
                    body(r * 2 + k, r, k)

        @block.sync
        def _(sp):
            for n, w in enumerate(w_proj):
                sp.dma_start(proj_raw[:, n * DP:(n + 1) * DP], w).then_inc(consts_in, 16)
            sp.dma_start(proj_raw[:, UW:PW], w_g).then_inc(consts_in, 16)

            def body(q, r, k):
                sp.dma_start(x_in_sb[:, k], x_tiles[:, bass.ds(q * GT, GT), :]).then_inc(x_in[k], 16)
                for j in range(2):
                    e = q * 2 + j
                    sp.wait_ge(w_lo_done, q * 2 + 1)
                    if j == 0:
                        sp.wait_ge(mix_lo_done, 1)
                    else:
                        sp.wait_ge(split_lo, 3)
                        sp.wait_ge(hb_ready, 1)
                    for m, w in enumerate((w1, w3)):
                        sp.dma_start(ew_raw[:, j, m * HID:(m + 1) * HID],
                                     w[bass.ds(e, 1)].rearrange("a p h -> p (a h)")).then_inc(w_in[j], 16)
                    sp.dma_start(ew_raw[:, j, 2 * HID:EW].rearrange("p (c d) -> p c d", c=NC),
                                 w2[bass.ds(e, 1)].rearrange("a (c p) d -> p (a c) d", p=P)).then_inc(w_in[j], 16)
                    if j == 0:
                        sp.wait_ge(xn_done, q * GT + GT)
                        sp.dma_start(xn_tiles[:, bass.ds(q * GT, GT), :], xn[:, k]).then_inc(xn_out[k], 16)

            groups(sp, body)
            sp.wait_ge(filled, 1)
            sp.wait_ge(made, 5)
            sp.dma_start(rows_dram[IDLE:IDLE + P, :], pad_row[:]).then_inc(pad_out, 16)
            sp.wait_ge(planned, 3)
            for e in range(E):
                start = sp.value_load(plan[0:1, 2 * J + e:2 * J + e + 1], min_val=0, max_val=IDLE - P)
                sp.dma_start(rows_dram[bass.ds(start, P), :], pad_row[:]).then_inc(pad_out, 16)
            sp.wait_ge(pad_out, 16 * (E + 1))
            for k in range(2):
                sp.wait_ge(xn_out[k], 16 * (NG // 2) + 16)

        @block.gpsimd
        def _(pool):
            pool.memset(pad_row[:], 0.0).then_inc(filled, 1)
            pool.memset(half_power[:], -0.5).then_inc(filled, 1)
            pool.memset(ones[:], 1.0).then_inc(filled, 1)
            pool.memset(ones_bf[:], 1.0).then_inc(filled, 1)
            pool.memset(keep_sum[:], 1.0).then_inc(filled, 1)
            pool.memset(mask[:], 0.0).then_inc(filled, 1)
            pool.wait_ge(filled, 6)
            pool.affine_select(out=ident[:], in_=ones[:], compare_op=ALU.is_equal, fill=0.0, base=0,
                               pattern=[[-1, P]], channel_multiplier=1).then_inc(made, 1)
            pool.affine_select(out=before[:], in_=ones_bf[:], compare_op=ALU.is_gt, fill=0.0, base=0,
                               pattern=[[1, P]], channel_multiplier=-1).then_inc(made, 1)
            pool.iota(first_key[:], [[-1, E]], base=E, channel_multiplier=0,
                      allow_small_or_imprecise_dtypes=True).then_inc(made, 1)
            pool.iota(region[:], [[REG, E]], base=0, channel_multiplier=0,
                      allow_small_or_imprecise_dtypes=True).then_inc(made, 1)
            pool.iota(pad_row[:, D:ROW].bitcast(U32), [[0, 1]], base=DUMP, channel_multiplier=1).then_inc(made, 1)
            pool.iota(dest[:], [[TOK, K], [P, GT]], base=0, channel_multiplier=1,
                      allow_small_or_imprecise_dtypes=True).then_inc(made, 1)
            pool.iota(steps[:], [[1, J]], base=0, channel_multiplier=0,
                      allow_small_or_imprecise_dtypes=True).then_inc(made, 1)
            pool.memset(keep_sum[:, :, 0:1], 0.0).then_inc(made, 1)

            def inverse_deviation(q):
                pool.wait_ge(var_done, q + 1)
                pool.wait_ge(xn_done, q * GT)
                pool.tensor_tensor(rstd[:], var_eps[:], half_power[:], ALU.pow).then_inc(rstd_done, 1)

            inverse_deviation(0)
            for q in range(NG):
                k = q % 2
                pool.wait_ge(idx_done, q + 2)
                pool.wait_ge(dest_done, q + 1)
                for n in range(K * GT):
                    i, slot = n // K, n % K
                    pool.wait_ge(row1_done if slot else row0_done, q * GT + i + 1 + slot)
                    at = slot * GT + i
                    pool.indirect_dma_start(
                        out=rows_dram[:, :],
                        out_offset=bass.IndirectOffsetOnAxis(ap=slot_row[:, k, at:at + 1], axis=0),
                        in_=rows[:, k, at, :], in_offset=None).then_inc(sent[k], 16)
                    if n == 3 and q:
                        pool.wait_ge(sent[1 - k], 16 * K * GT * ((q + 1) // 2))
                        pool.sem_inc(rows_free, 1)
                    if n == 10 and q + 1 < NG:
                        inverse_deviation(q + 1)
            for k in range(2):
                pool.wait_ge(sent[k], 16 * K * GT * (NG // 2))

        @block.scalar
        def _(act):
            act.dma_start(gate_raw, w_gate).then_inc(consts_in, 16)
            act.dma_start(gbias_raw[:], b_gate.unsqueeze(0)).then_inc(consts_in, 16)
            act.dma_start(g_bias[:], b_g.partition_broadcast(P)).then_inc(consts_in, 16)
            act.dma_start(sums, mix_sums).then_inc(consts_in, 16)
            for n, b in enumerate(b_proj):
                act.dma_start(pbias[n % 2:n % 2 + 1, (n // 2) * DP:(n // 2 + 1) * DP],
                              b.unsqueeze(0)).then_inc(consts_in, 16)
            act.dma_start(mix_raw, mix).then_inc(mix_in, 16)
            act.preload_act_table(ACT.Exp)
            act.wait_ge(consts_in, 16 * 13)
            act.activation(proj_hi[:], proj_raw, ACT.Copy).then_inc(split_hi, 1)
            act.activation(gate_hi[:], gate_raw, ACT.Copy).then_inc(split_hi, 1)
            act.activation(gbias_hi[:], gbias_raw[:], ACT.Copy).then_inc(split_hi, 1)
            act.wait_ge(filled, 6)
            act.activation(ones_r[:], ones[0:1, :], ACT.Copy).then_inc(split_hi, 1)
            act.wait_ge(mix_in, 16)
            act.activation(mix_hi[:], mix_raw, ACT.Copy).then_inc(mix_hi_done, 1)

            def body(q, r, k):
                for half in range(2):
                    act.wait_ge(xt_ready, q * 2 + half + 1)
                    act.activation(xt_hi[:, half], xt_bank[half][:], ACT.Copy).then_inc(xt_hi_done, 1)
                for i in range(GT):
                    act.wait_ge(u_ready, q * GT + i + 1)
                    act.activation(u_hi[:, i], u_bank[i % 2][:, 0:UW], ACT.Copy).then_inc(u_hi_done, 1)
                act.wait_ge(gap_done, q + 1)
                act.activation(ratio[:], gap[:], ACT.Exp).then_inc(exp_done, 1)
                act.wait_ge(weight_done, q * 2 + 2)
                act.wait_ge(rows_free, q + 1)
                for i in range(GT):
                    act.activation(rows[:, k, GT + i, 0:D], xn[:, k, i], ACT.Copy,
                                   scale=weight[:, 1, i:i + 1]).then_inc(row1_done, 1)
                for half in range(2):
                    act.wait_ge(ht_ready, q * 2 + half + 1)
                    act.activation(ht_hi[:, half], xt_bank[half][:], ACT.Copy).then_inc(ht_hi_done, 1)
                for j in range(2):
                    act.wait_ge(w_in[j], q * 48 + 48)
                    act.activation(ew_hi[:, bass.ds((q * 2 + j) * EW, EW)], ew_raw[:, j], ACT.Copy
                                   ).then_inc(w_hi_done, 1)
                for half in range(2):
                    act.wait_ge(gate_ready, q * 2 + half + 1)
                    act.activation(gate_bank[:], gate_bank[:], ACT.Tanh, scale=0.5).then_inc(tanh_done, 1)

            groups(act, body)

        @block.vector
        def _(dve):
            dve.wait_ge(split_hi, 3)
            dve.tensor_tensor(proj_lo[:], proj_raw, proj_hi[:].bitcast(F32), ALU.subtract).then_inc(split_lo, 1)
            dve.tensor_tensor(gate_lo[:], gate_raw, gate_hi[:].bitcast(F32), ALU.subtract).then_inc(split_lo, 1)
            dve.tensor_tensor(gbias_lo[:], gbias_raw[:], gbias_hi[:].bitcast(F32), ALU.subtract
                              ).then_inc(split_lo, 1)
            dve.wait_ge(made, 8)

            for k in range(2):
                dve.sem_inc(xn_out[k], 16)
            dve.sem_inc(rows_free, 2)
            dve.sem_inc(exp_done, 1)
            dve.sem_inc(row1_done, 1)
            dve.sem_inc(w_lo_done, 1)
            NR = 17

            def body(q, r, k):
                done = [0]

                def chain(ins):
                    ins.then_inc(route, 1)
                    done[0] += 1
                    dve.wait_ge(route, q * NR + done[0])

                dve.wait_ge(x_in[k], r * 16 + 16)
                for i in range(GT):
                    dve.bn_stats(stats[:, i], x_in_sb[:, k, i]).then_inc(stats_done, 1)
                dve.wait_ge(stats_done, q * GT + GT)
                dve.sem_inc(stats_seen, 1)
                for i in range(GT):
                    dve.bn_aggr(moments[:, i], stats[:, i]).then_inc(moments_done, 1)
                dve.wait_ge(moments_done, q * GT + GT)
                dve.tensor_scalar(var_eps[:], moments[:, :, 1], EPS, None, ALU.add).then_inc(var_done, 1)
                dve.wait_ge(rstd_done, q + 1)
                dve.wait_ge(xn_out[k], r * 16 + 16)
                for i in range(GT):
                    dve.tensor_scalar(xn[:, k, i], x_in_sb[:, k, i], moments[:, i, 0:1], rstd[:, i:i + 1],
                                      ALU.subtract, ALU.mult).then_inc(xn_done, 1)
                for half in range(2):
                    dve.wait_ge(xt_hi_done, q * 2 + half + 1)
                    dve.tensor_tensor(xt_lo[:, half], xt_bank[half][:], xt_hi[:, half].bitcast(F32),
                                      ALU.subtract).then_inc(xt_lo_done, 1)
                for i in range(GT):
                    dve.wait_ge(u_hi_done, q * GT + i + 1)
                    dve.tensor_tensor(logits[:, i], u_bank[i % 2][:, UW:PW], g_bias[:], ALU.add
                                      ).then_inc(logits_done, 1)
                    dve.tensor_tensor(u_lo[:, i], u_bank[i % 2][:, 0:UW], u_hi[:, i].bitcast(F32),
                                      ALU.subtract).then_inc(u_free, 1)
                dve.wait_ge(logits_done, q * GT + GT)
                for s, l in enumerate((logits, logits2)):
                    chain(dve.tensor_reduce(best[:, s], l[:], X, ALU.max))
                    chain(dve.tensor_tensor(key[:, 0], l[:], best[:, s].unsqueeze(2).broadcast_to([P, GT, E]),
                                            ALU.is_equal))
                    chain(dve.tensor_tensor(key[:, 1], key[:, 0],
                                            first_key[:].unsqueeze(1).broadcast_to([P, GT, E]), ALU.mult))
                    chain(dve.tensor_reduce(best_key[:, s], key[:, 1], X, ALU.max))
                    chain(dve.tensor_tensor(chosen[:, s], key[:, 1],
                                            best_key[:, s].unsqueeze(2).broadcast_to([P, GT, E]), ALU.is_equal))
                    if s == 0:
                        chain(dve.scalar_tensor_tensor(out=logits2[:], in0=chosen[:, 0], scalar=LOWEST,
                                                       in1=logits[:], op0=ALU.mult, op1=ALU.add))
                        dve.wait_ge(exp_done, q + 1)
                dve.tensor_tensor(gap[:], best[:, 1], best[:, 0], ALU.subtract).then_inc(gap_done, 1)
                chain(dve.tensor_tensor(mask[:, :, 1:GT + 1], chosen[:, 0].rearrange("p i e -> p e i"),
                                        chosen[:, 1].rearrange("p i e -> p e i"), ALU.add))
                dve.tensor_tensor_scan(prefix[:].rearrange("p e i -> p (e i)"),
                                       keep_sum[:].rearrange("p e i -> p (e i)"),
                                       mask[:].rearrange("p e i -> p (e i)"), 0.0, ALU.mult, ALU.add
                                       ).then_inc(prefix_done, 1)
                dve.wait_ge(exp_done, q + 2)
                chain(dve.tensor_scalar(denom[:], ratio[:], 1.0, None, ALU.add))
                dve.wait_ge(row1_done, q * GT + 1)
                dve.reciprocal(weight[:, 0], denom[:]).then_inc(weight_done, 1)
                dve.wait_ge(weight_done, q * 2 + 1)
                dve.tensor_tensor(weight[:, 1], ratio[:], weight[:, 0], ALU.mult).then_inc(weight_done, 1)
                dve.wait_ge(rows_free, q + 1)
                for i in range(GT):
                    dve.tensor_scalar(rows[:, k, i, 0:D], xn[:, k, i], weight[:, 0, i:i + 1], None,
                                      ALU.mult).then_inc(row0_done, 1)
                chain(dve.tensor_copy(rows[:, k, :, D].bitcast(U32), dest[:]))
                dve.tensor_scalar(dest[:], dest[:], float(GT * P), None, ALU.add).then_inc(dest_done, 1)
                dve.wait_ge(pos_ready, q + 1)
                chain(dve.tensor_tensor(position[:], pos_bank[:, 0:E * GT].rearrange("p (e i) -> p e i", e=E),
                                        region[:].unsqueeze(2).broadcast_to([P, E, GT]), ALU.add))
                chain(dve.tensor_tensor(picked[:], chosen[:],
                                        position[:].rearrange("p e i -> p i e").unsqueeze(1)
                                        .broadcast_to([P, K, GT, E]), ALU.mult))
                with nc.allow_low_precision(reason="a whole number below 2^24, summed in float32"):
                    dve.tensor_reduce(slot_row[:, k], picked[:].rearrange("p s i e -> p (s i) e"), X, ALU.add
                                      ).then_inc(idx_done, 1)
                chain(dve.tensor_copy(mask[:, :, 0], prefix[:, :, GT]))
                assert done[0] == NR, done[0]

                for tb in range(2):
                    dve.wait_ge(h_ready, q * 2 + tb + 1)
                    if tb == 0:
                        dve.wait_ge(hb_done, 2)
                    dve.tensor_tensor(h[:].rearrange("p (b t) d -> p t b d", t=2)[:, tb],
                                      h_bank[tb][:].rearrange("p (b d) -> p b d", b=GB),
                                      h_bias[:, tb].unsqueeze(1).broadcast_to([P, GB, D]), ALU.add
                                      ).then_inc(h_free, 1)
                for half in range(2):
                    dve.wait_ge(ht_hi_done, q * 2 + half + 1)
                    dve.tensor_tensor(ht_lo[:, half], xt_bank[half][:], ht_hi[:, half].bitcast(F32),
                                      ALU.subtract).then_inc(xt_free, 1)
                for j in range(2):
                    dve.wait_ge(w_hi_done, q * 2 + j + 1)
                    dve.tensor_tensor(ew_lo[:, bass.ds((q * 2 + j) * EW, EW)], ew_raw[:, j],
                                      ew_hi[:, bass.ds((q * 2 + j) * EW, EW)].bitcast(F32), ALU.subtract
                                      ).then_inc(w_lo_done, 1)
                for half in range(2):
                    dve.wait_ge(tanh_done, q * 2 + half + 1)
                    dve.scalar_tensor_tensor(
                        out=gated[:, bass.ds(q * GT + half * HT4, HT4), :].rearrange("p i d -> p (i d)"),
                        in0=gate_bank[:], scalar=1.0,
                        in1=h[:, half * HT4:(half + 1) * HT4].rearrange("p i d -> p (i d)"),
                        op0=ALU.add, op1=ALU.mult).then_inc(gate_free, 1)

            dve.wait_ge(mix_hi_done, 1)
            dve.tensor_tensor(mix_lo[:], mix_raw, mix_hi[:].bitcast(F32), ALU.subtract).then_inc(mix_lo_done, 1)
            dve.wait_ge(hb_ready, 1)
            dve.tensor_copy(h_bias[:].rearrange("p t d -> p (t d)"), gate_bank[:, 0:2 * D]).then_inc(hb_done, 2)
            groups(dve, body)

            done = [0]

            def then(ins):
                ins.then_inc(planning, 1)
                done[0] += 1
                dve.wait_ge(planning, done[0])

            dve.wait_ge(count_ready, 1)
            then(dve.tensor_copy(count[:], pos_bank[0:1, 0:E]))
            then(dve.tensor_scalar(padded[:], count[:], float(P - 1), None, ALU.add))
            then(dve.tensor_scalar(tiles_i[:], padded[:], 7, None, ALU.arith_shift_right))
            then(dve.tensor_copy(tiles_f[:], tiles_i[:]))
            then(dve.tensor_tensor_scan(tile_end[:], ones[0:1, 0:E], tiles_f[:], 0.0, ALU.mult, ALU.add))
            then(dve.tensor_scalar(jump[:], tiles_f[:], float(-P), float(REG), ALU.mult, ALU.add))
            then(dve.tensor_tensor(passed, steps[:].unsqueeze(2).broadcast_to([1, J, E]),
                                   tile_end[:].unsqueeze(1).broadcast_to([1, J, E]), ALU.is_ge))
            then(dve.tensor_tensor(jumped, passed, jump[:].unsqueeze(1).broadcast_to([1, J, E]),
                                   ALU.mult))
            then(dve.tensor_reduce(plan_f[:, 0], jumped, X, ALU.add))
            then(dve.tensor_reduce(plan_f[:, 1], passed, X, ALU.add))
            then(dve.scalar_tensor_tensor(out=plan_g[:], in0=steps[:], scalar=float(P), in1=plan_f[:, 0],
                                          op0=ALU.mult, op1=ALU.add))
            dve.tensor_scalar(plan[:, 0:J], plan_g[:], float(IDLE), None, ALU.min).then_inc(planned, 1)
            dve.tensor_scalar(plan[:, J:2 * J], plan_f[:, 1], float(E - 1), float(EW), ALU.min, ALU.mult
                              ).then_inc(planned, 1)
            dve.tensor_tensor(plan[:, 2 * J:], count[:], region[0:1, :], ALU.add).then_inc(planned, 1)

        @block.tensor
        def _(pe):
            def product(to, lhs, rhs, first=True, last=True):
                (a_hi, a_lo), (b_hi, b_lo) = lhs, rhs
                pe.matmul(to, a_hi, b_hi, start=first, stop=False, skip_group_check=True)
                pe.matmul(to, a_hi, b_lo, start=False, stop=False, skip_group_check=True)
                return pe.matmul(to, a_lo, b_hi, start=False, stop=last, skip_group_check=True)

            pe.wait_ge(made, 1)
            pe.sem_inc(xt_free, 2)
            pe.sem_inc(u_free, 2)
            pe.sem_inc(gate_free, 1)
            pe.sem_inc(h_free, 2)
            pe.sem_inc(idx_done, 1)

            def mixing(q, tb):
                pe.wait_ge(h_free, q * 2 + 2)
                halves = [(0, 1), (1, 0)] if tb else [(0, 0)]
                for i in range(SC):
                    to = h_bank[tb][:].rearrange("p (b s c) -> p b s c", b=GB, s=SC)[:, :, i]
                    terms = [(src, blk, part) for src, blk in halves for part in range(2)]
                    for n, (src, blk, part) in enumerate(terms):
                        at = ((i * 2 + part) * 2 + blk) * P
                        col = (i * 2 + part) * DP
                        u = [t[:].rearrange("p (b t) c -> p t b c", t=2)[:, src, :, col:col + DP]
                             for t in (u_hi, u_lo)]
                        mm = product(to, (mix_hi[:, at:at + P], mix_lo[:, at:at + P]), u,
                                     n == 0, n == len(terms) - 1)
                mm.then_inc(h_ready, 1)

            def body(q, r, k):
                for half in range(2):
                    pe.wait_ge(xn_done, q * GT + (half + 1) * HT4)
                    pe.wait_ge(xt_free, q * 2 + half + 1)
                    for i in range(HT4):
                        t = pe.transpose(xt_bank[half][:, i * P:(i + 1) * P], xn[:, k, half * HT4 + i], ident[:])
                    t.then_inc(xt_ready, 1)
                for i in range(GT):
                    half, at = i // HT4, (i % HT4) * P
                    pe.wait_ge(xt_lo_done, q * 2 + half + 1)
                    pe.wait_ge(u_free, q * GT + i + 1)
                    product(u_bank[i % 2][:, 0:PW], (xt_hi[:, half, at:at + P], xt_lo[:, half, at:at + P]),
                            (proj_hi[:], proj_lo[:])).then_inc(u_ready, 1)
                pe.wait_ge(u_free, q * GT + GT + 2)
                if k == 0:
                    pe.wait_ge(mix_lo_done, 1)
                mixing(q, 0)
                pe.wait_ge(prefix_done, q + 1)
                pe.wait_ge(idx_done, q + 1)
                to = pos_bank[:, 0:E * GT].rearrange("p (e i) -> p e i", e=E)
                pe.matmul(to, before[:], mask[:, :, 1:GT + 1], start=True, stop=False)
                pe.matmul(to, ones_bf[:], prefix[:, :, 0:GT], start=False, stop=True).then_inc(pos_ready, 1)
                mixing(q, 1)
                for half in range(2):
                    pe.wait_ge(h_free, q * 2 + 4)
                    for i in range(HT4):
                        t = pe.transpose(xt_bank[half][:, i * P:(i + 1) * P], h[:, half * HT4 + i], ident[:])
                    t.then_inc(ht_ready, 1)
                for half in range(2):
                    pe.wait_ge(xt_free, q * 2 + half + 3)
                    pe.wait_ge(gate_free, q * 2 + half + 1)
                    to = gate_bank[:].rearrange("p (i d) -> p i d", i=HT4)
                    for n, b in enumerate((gbias_hi, gbias_lo)):
                        pe.matmul(to, ones_r[:], b[:].unsqueeze(1).broadcast_to([1, HT4, D]),
                                  start=(n == 0), stop=False, skip_group_check=True)
                    for i in range(HT4):
                        at = i * P
                        mm = product(gate_bank[:, i * D:(i + 1) * D],
                                     (ht_hi[:, half, at:at + P], ht_lo[:, half, at:at + P]),
                                     (gate_hi[:], gate_lo[:]), False, i == HT4 - 1)
                    mm.then_inc(gate_ready, 1)

            pe.wait_ge(consts_in, 16 * 13)
            for tb in range(2):
                for i in range(SC):
                    mm = pe.matmul(gate_bank[:, tb * D + i * DP:tb * D + (i + 1) * DP],
                                   sums[:, i * S + tb * P:i * S + (tb + 1) * P],
                                   pbias[:, i * DP:(i + 1) * DP], start=True, stop=True)
            mm.then_inc(hb_ready, 1)
            pe.wait_ge(hb_done, 2)
            pe.wait_ge(split_lo, 3)
            pe.wait_ge(split_hi, 4)
            pe.wait_ge(made, 8)
            groups(pe, body)
            pe.wait_ge(route, NG * 17)
            pe.wait_ge(idx_done, NG + 1)
            pe.matmul(pos_bank[:, 0:E], ones_bf[:], mask[:, :, 0], start=True, stop=True).then_inc(count_ready, 1)


def experts(nc, sem, banks, ident, ew_hi, ew_lo, plan, rows_dram, y_dram, x_tiles, xn_tiles,
            x_all, xn_all, tail_in):
    ctx = ExitStack()
    with ctx:
        def sb(name, shape, dt):
            return ctx.enter_context(nc.sbuf_tensor(name, shape, dt))

        row = sb("row", [P, RING, ROW], F32)
        xt_hi = sb("row_t_hi", [P, 2, P], F32R)
        xt_lo = sb("row_t_lo", [P, 2, P], F32R)
        act_a = sb("act_a", [P, 2, HID], F32)
        hid = sb("hid", [P, 2, HID], F32)
        ht_hi = sb("hid_t_hi", [P, 2, HID], F32R)
        ht_lo = sb("hid_t_lo", [P, 2, HID], F32R)
        y = sb("y", [P, RING, D], F32)

        a_bank, c_bank, ht_bank = banks[0:2], banks[2:4], banks[4:6]
        xt_bank, y_bank = banks[6], banks[7]

        row_in = [sem(f"row_in{k}") for k in range(RING)]
        y_out = [sem(f"y_out{k}") for k in range(RING)]
        xt_ready, xt_hi_done, xt_lo_done = sem("e_xt_ready"), sem("e_xt_hi_done"), sem("e_xt_lo_done")
        a_ready, silu_done = sem("a_ready"), sem("silu_done")
        c_ready, hid_done = sem("c_ready"), sem("hid_done")
        ht_ready, ht_hi_done, ht_lo_done = sem("e_ht_ready"), sem("e_ht_hi_done"), sem("e_ht_lo_done")
        y_ready, y_done, y_seen = sem("y_ready"), sem("y_done"), sem("y_seen")

        block = ctx.enter_context(nc.Block())

        def tiles(eng, step, head=1):
            for j in range(head * RING):
                step(j, j // RING, j % RING)
            with eng.Fori(head, J // RING - 1) as g:
                for k in range(RING):
                    step(g * RING + k, g, k)
            for k in range(RING):
                step(J - RING + k, J // RING - 1, k)

        def at(j, back=0):
            return not isinstance(j, int) or 0 <= j - back < J

        @block.sync
        def _(sp):
            def step(j, g, k):
                start = sp.value_load(plan[0:1, bass.ds(j, 1)], min_val=0, max_val=IDLE)
                if not isinstance(g, int) or g:
                    sp.wait_ge(y_out[k], g * 16)
                sp.dma_start(row[:, k], rows_dram[bass.ds(start, P), :]).then_inc(row_in[k], 16)

            tiles(sp, step)

        @block.gpsimd
        def _(pool):
            def step(k, g):
                pool.wait_ge(y_done, g * RING + k + 1)
                pool.sem_inc(y_seen, 1)
                pool.indirect_dma_start(
                    out=y_dram[:, :],
                    out_offset=bass.IndirectOffsetOnAxis(ap=row[:, k, D:ROW].bitcast(U32), axis=0),
                    in_=y[:, k], in_offset=None,
                    bounds_check=DUMP - 1, oob_is_err=False).then_inc(y_out[k], 16)

            with pool.Fori(0, J // RING) as g:
                for k in range(RING):
                    step(k, g)
            for k in range(RING):
                pool.wait_ge(y_out[k], 16 * (J // RING))

        @block.scalar
        def _(act):
            act.preload_act_table(ACT.Silu)
            act.dma_start(x_all[:], x_tiles).then_inc(tail_in, 16)
            act.dma_start(xn_all[:], xn_tiles).then_inc(tail_in, 16)

            def row_hi(j):
                act.wait_ge(xt_ready, j + 1)
                act.activation(xt_hi[:, j_parity(j)], xt_bank[:, 0:P], ACT.Copy).then_inc(xt_hi_done, 1)

            parity = [0]

            def j_parity(j):
                return parity[0]

            def step(j, g, k):
                if isinstance(j, int) and j == 0:
                    parity[0] = 0
                    row_hi(0)
                if at(j, -1):
                    parity[0] = (k + 1) % 2
                    row_hi(j + 1)
                act.wait_ge(a_ready, j + 1)
                if not isinstance(j, int) or j >= 2:
                    act.wait_ge(hid_done, j - 1)
                act.activation(act_a[:, k % 2], a_bank[k % 2][:], ACT.Silu).then_inc(silu_done, 1)
                if at(j, 1):
                    hidden_hi(j - 1, (k - 1) % 2)

            def hidden_hi(j, b):
                act.wait_ge(ht_ready, j + 1)
                if not isinstance(j, int) or j >= 2:
                    act.wait_ge(y_ready, j - 1)
                act.activation(ht_hi[:, b], ht_bank[b][:], ACT.Copy).then_inc(ht_hi_done, 1)

            tiles(act, step)
            hidden_hi(J - 1, (J - 1) % 2)

        @block.vector
        def _(dve):
            def row_lo(j, b):
                dve.wait_ge(xt_hi_done, j + 1)
                dve.tensor_tensor(xt_lo[:, b], xt_bank[:, 0:P], xt_hi[:, b].bitcast(F32), ALU.subtract
                                  ).then_inc(xt_lo_done, 1)

            def hidden_lo(j, b):
                dve.wait_ge(ht_hi_done, j + 1)
                dve.tensor_tensor(ht_lo[:, b], ht_bank[b][:], ht_hi[:, b].bitcast(F32), ALU.subtract
                                  ).then_inc(ht_lo_done, 1)

            def result(j, g, k):
                dve.wait_ge(y_ready, j + 1)
                if not isinstance(g, int) or g:
                    dve.wait_ge(y_out[k], g * 16)
                dve.tensor_reduce(y[:, k], y_bank[:, 0:2 * D].rearrange("p (a d) -> p d a", a=2), X, ALU.add
                                  ).then_inc(y_done, 1)

            def step(j, g, k):
                if isinstance(j, int) and j == 0:
                    row_lo(0, 0)
                if at(j, -1):
                    row_lo(j + 1, (k + 1) % 2)
                dve.wait_ge(silu_done, j + 1)
                dve.wait_ge(c_ready, j + 1)
                if not isinstance(j, int) or j >= 2:
                    dve.wait_ge(ht_ready, j - 1)
                dve.tensor_tensor(hid[:, k % 2], c_bank[k % 2][:], act_a[:, k % 2], ALU.mult
                                  ).then_inc(hid_done, 1)
                if at(j, 1):
                    hidden_lo(j - 1, (k - 1) % 2)
                if at(j, 2):
                    result(j - 2, g if k >= 2 else g - 1, (k - 2) % RING)

            tiles(dve, step, head=2)
            hidden_lo(J - 1, (J - 1) % 2)
            result(J - 2, J // RING - 1, RING - 2)
            result(J - 1, J // RING - 1, RING - 1)

        @block.tensor
        def _(pe):
            def transpose_row(j, g, k):
                pe.wait_ge(row_in[k], g * 16 + 16)
                if not isinstance(j, int) or j:
                    pe.wait_ge(xt_lo_done, j)
                pe.transpose(xt_bank[:, 0:P], row[:, k, 0:D], ident[:]).then_inc(xt_ready, 1)

            column = {}

            def column_of(j, b):
                column[b] = pe.value_load(plan[0:1, bass.ds(j + J, 1)], min_val=0, max_val=(E - 1) * EW)

            def up(j, b):
                pe.wait_ge(xt_lo_done, j + 1)
                for m, (bank, free, ready) in enumerate(((a_bank[b], silu_done, a_ready),
                                                         (c_bank[b], hid_done, c_ready))):
                    if not isinstance(j, int) or j >= 2:
                        pe.wait_ge(free, j - 1)
                    w = [t[:, bass.ds(column[b] + m * HID, HID)] for t in (ew_hi, ew_lo)]
                    pe.matmul(bank[:], xt_hi[:, b], w[0], start=True, stop=False)
                    pe.matmul(bank[:], xt_hi[:, b], w[1], start=False, stop=False)
                    pe.matmul(bank[:], xt_lo[:, b], w[0], start=False, stop=True).then_inc(ready, 1)

            def transpose_hidden(j, b):
                pe.wait_ge(hid_done, j + 1)
                if not isinstance(j, int) or j >= 2:
                    pe.wait_ge(ht_lo_done, j - 1)
                for c in range(NC):
                    t = pe.transpose(ht_bank[b][:, c * P:(c + 1) * P], hid[:, b, c * P:(c + 1) * P], ident[:])
                t.then_inc(ht_ready, 1)

            def down(j, b, col):
                pe.wait_ge(ht_lo_done, j + 1)
                if not isinstance(j, int) or j:
                    pe.wait_ge(y_done, j)
                for c in range(NC):
                    w = [t[:, bass.ds(col + (2 * HID + c * D), D)] for t in (ew_hi, ew_lo)]
                    hi, lo = ht_hi[:, b, c * P:(c + 1) * P], ht_lo[:, b, c * P:(c + 1) * P]
                    pe.matmul(y_bank[:, 0:D], hi, w[0], start=(c == 0), stop=False, skip_group_check=True)
                    pe.matmul(y_bank[:, D:2 * D], hi, w[1], start=False, stop=False, skip_group_check=True)
                    mm = pe.matmul(y_bank[:, 0:D], lo, w[0], start=False, stop=(c == NC - 1),
                                   skip_group_check=True)
                mm.then_inc(y_ready, 1)

            def second_column(j):
                return pe.value_load(plan[0:1, bass.ds(j + J, 1)], min_val=0, max_val=(E - 1) * EW)

            def step(j, g, k):
                if isinstance(j, int) and j == 0:
                    transpose_row(0, 0, 0)
                column_of(j, k % 2)
                if at(j, -1):
                    transpose_row(j + 1, g if k < RING - 1 else g + 1, (k + 1) % RING)
                up(j, k % 2)
                if at(j, 1):
                    transpose_hidden(j - 1, (k - 1) % 2)
                if at(j, 2):
                    down(j - 2, k % 2, second_column(j - 2))

            tiles(pe, step)
            transpose_hidden(J - 1, (J - 1) % 2)
            down(J - 2, (J - 2) % 2, second_column(J - 2))
            down(J - 1, (J - 1) % 2, second_column(J - 1))


def combine(nc, sem, gated, x_all, xn_all, tail_in, y_tiles, out_tiles):
    CT = 4
    ctx = ExitStack()
    with ctx:
        def sb(name, shape, dt):
            return ctx.enter_context(nc.sbuf_tensor(name, shape, dt))

        y = sb("y_pair", [P, 2, K, CT * D], F32)
        total = sb("total", [P, 2, CT * D], F32)
        ffn = sb("ffn", [P, 2, CT * D], F32)
        silu = sb("silu", [P, 2, CT * D], F32)
        res = sb("res", [P, 2, CT * D], F32)
        y_in = [sem(f"y_in{k}") for k in range(2)]
        stored = [sem(f"stored{k}") for k in range(2)]
        sum_done, ffn_done, silu_ready = sem("sum_done"), sem("ffn_done"), sem("silu_ready")
        prod_done, res_done = sem("prod_done"), sem("res_done")
        n_chunks = NT // CT
        block = ctx.enter_context(nc.Block())

        def flat(t, c):
            return t[:, bass.ds(c * CT, CT), :].rearrange("p i d -> p (i d)")

        def chunks(eng, body):
            with eng.Fori(0, n_chunks // 2) as r:
                for k in range(2):
                    body(r * 2 + k, r, k)

        @block.sync
        def _(sp):
            def body(c, r, k):
                sp.wait_ge(sum_done, r * 2 + 1)
                for s in range(K):
                    sp.dma_start(y[:, k, s].rearrange("p (i d) -> p i d", i=CT),
                                 y_tiles[:, s, bass.ds(c * CT, CT), :]).then_inc(y_in[k], 16)

            chunks(sp, body)

        @block.gpsimd
        def _(pool):
            pass

        @block.tensor
        def _(pe):
            pass

        @block.scalar
        def _(act):
            act.preload_act_table(ACT.Silu)

            def store(c, k):
                act.wait_ge(res_done, c + 1)
                act.dma_start(out_tiles[:, bass.ds(c * CT, CT), :],
                              res[:, k].rearrange("p (i d) -> p i d", i=CT)).then_inc(stored[k], 16)

            def body(c, r, k):
                act.wait_ge(ffn_done, c + 1)
                act.activation(silu[:, k], ffn[:, k], ACT.Silu).then_inc(silu_ready, 1)
                store(c, k)

            chunks(act, body)
            for k in range(2):
                act.wait_ge(stored[k], 16 * (n_chunks // 2) + 16)

        @block.vector
        def _(dve):
            dve.wait_ge(tail_in, 32)
            dve.sem_inc(sum_done, 1)
            dve.sem_inc(silu_ready, 1)
            for k in range(2):
                dve.sem_inc(stored[k], 16)

            def body(c, r, k):
                dve.wait_ge(y_in[k], r * 32 + 32)
                dve.tensor_tensor(total[:, k], y[:, k, 0], y[:, k, 1], ALU.add).then_inc(sum_done, 1)
                dve.wait_ge(sum_done, c + 2)
                dve.wait_ge(silu_ready, c + 1)
                dve.tensor_tensor(ffn[:, k], total[:, k], flat(xn_all, c), ALU.add).then_inc(ffn_done, 1)
                dve.wait_ge(silu_ready, c + 2)
                dve.tensor_tensor(total[:, k], silu[:, k], flat(gated, c), ALU.mult).then_inc(prod_done, 1)
                dve.wait_ge(prod_done, c + 1)
                dve.wait_ge(stored[k], r * 16 + 16)
                dve.scalar_tensor_tensor(out=res[:, k], in0=total[:, k], scalar=0.5, in1=flat(x_all, c),
                                         op0=ALU.mult, op1=ALU.add).then_inc(res_done, 1)

            chunks(dve, body)


_INS = ["L0_attn_x", "L0_attn_W_re0", "L0_attn_b_re0", "L0_attn_W_im0", "L0_attn_b_im0", "L0_attn_W_re1",
        "L0_attn_b_re1", "L0_attn_W_im1", "L0_attn_b_im1", "L0_attn_W_gate", "L0_attn_b_gate", "L0_ffn_Wg",
        "L0_ffn_bg", "L0_ffn_W1", "L0_ffn_W2", "L0_ffn_W3"]


def kernel(**inputs):
    import concourse.bacc as bacc
    from concourse.bass_utils import run_bass_kernel_spmd

    nc = bacc.Bacc("TRN2", target_bir_lowering=False, num_devices=1)
    blocks, sums = mixing_tables()
    arrays = {f"in_{name}": np.ascontiguousarray(inputs[name]) for name in _INS}
    arrays["mix_blocks"], arrays["mix_sums"] = blocks, sums
    args = [nc.dram_tensor(name, a.shape, mybir.dt.from_np(a.dtype), kind="ExternalInput").ap()
            for name, a in arrays.items()]
    args.append(nc.dram_tensor("out", (B, S, D), F32, kind="ExternalOutput").ap())
    build(nc, *args)
    r = run_bass_kernel_spmd(nc, [arrays], core_ids=[0])
    return r.results[0]["out"]
```

```python
from contextlib import ExitStack

import numpy as np

import concourse.bass as bass
import concourse.mybir as mybir

F32 = mybir.dt.float32
F32R = mybir.dt.float32r
BF16 = mybir.dt.bfloat16
I32 = mybir.dt.int32
U32 = mybir.dt.uint32
ALU = mybir.AluOpType
ACT = mybir.ActivationFunctionType
X = mybir.AxisListType.X

P = 128
B, S, D = 16, 256, 128
TOK = B * S
NT = TOK // P
E, K, HID = 8, 2, 512
NC = HID // P
SC = 2
DP = D // SC
UW = 2 * SC * DP
GT = 8
NG = NT // GT
GB = GT // 2
HT4 = GT // 2
ROW = D + 1
REG = TOK + P
IDLE = E * REG
J = K * TOK // P + E
TURN = 8
TURNS = J // TURN
PART = NT // (TURNS - 1)
EC = 3 * NC
EW = EC * P
DUMP = K * TOK
EPS = 1e-5
LOWEST = -3.0e38
R_VALS = np.linspace(0.999, 0.9, SC)
TH_VALS = np.linspace(0.01, 1.0, SC)


def mixing_tables():
    blocks = np.zeros((P, SC, 2, 2, P), np.float64)
    sums = np.zeros((2, SC, S), np.float64)
    lag = np.arange(P)[None, :] - np.arange(P)[:, None]
    for i in range(SC):
        a = complex(np.complex64(float(R_VALS[i]) * np.exp(1j * float(TH_VALS[i]))))
        powers = float(np.float32(1.0 - float(R_VALS[i]))) * np.exp(np.log(a) * np.arange(S))
        for part, f in enumerate((powers.real, -powers.imag)):
            blocks[:, i, part, 0] = np.where(lag >= 0, f[np.maximum(lag, 0)], 0.0)
            blocks[:, i, part, 1] = f[lag + P]
            sums[part, i] = np.cumsum(f)
    return blocks.reshape(P, -1).astype(np.float32), sums.reshape(2, -1).astype(np.float32)


def build(nc, x, w_re0, b_re0, w_im0, b_im0, w_re1, b_re1, w_im1, b_im1, w_gate, b_gate,
          w_g, b_g, w1, w2, w3, mix, mix_sums, out):
    rows_dram = nc.dram_tensor("rows_dram", (IDLE + P, ROW), F32).ap()
    y_dram = nc.dram_tensor("y_dram", (K * TOK, D), F32).ap()
    xn_dram = nc.dram_tensor("xn_dram", (TOK, D), F32).ap()

    x_tiles = x.rearrange("b (h p) d -> p (b h) d", p=P)
    out_tiles = out.rearrange("b (h p) d -> p (b h) d", p=P)
    xn_tiles = xn_dram.rearrange("(n p) d -> p n d", p=P)
    y_tiles = y_dram.rearrange("(s n p) d -> p s n d", p=P, s=K)

    ctx = ExitStack()
    with ctx:
        def keep(name, shape, dt):
            return ctx.enter_context(nc.sbuf_tensor(name, shape, dt))

        def sem(name):
            return ctx.enter_context(nc.semaphore(name))

        gated = keep("gated", [P, NT, D], F32)
        ident = keep("ident", [P, P], F32)
        ew = keep("ew", [P, E * EC, 2, P], F32R)
        plan = keep("plan", [1, 2 * J + E], I32)
        banks = [ctx.enter_context(nc.psum_tensor(f"bank{i}", [P, 512], F32)) for i in range(8)]
        dispatch(nc, sem, banks, ident, ew, gated, plan, rows_dram, xn_tiles, x_tiles,
                 (w_re0, w_im0, w_re1, w_im1), (b_re0, b_im0, b_re1, b_im1), w_gate, b_gate,
                 w_g, b_g, w1, w2, w3, mix, mix_sums)
        x_all = keep("x_all", [P, NT, D], F32)
        xn_all = keep("xn_all", [P, NT, D], F32)
        tail_in = sem("tail_in")
        experts(nc, sem, banks, ident, ew, plan, rows_dram, y_dram, x_tiles, xn_tiles,
                x_all, xn_all, tail_in)
        combine(nc, sem, gated, x_all, xn_all, tail_in, y_tiles, out_tiles)


def dispatch(nc, sem, banks, ident, ew, gated, plan, rows_dram, xn_tiles, x_tiles,
             w_proj, b_proj, w_gate, b_gate, w_g, b_g, w1, w2, w3, mix, mix_sums):
    ctx = ExitStack()
    with ctx:
        def sb(name, shape, dt):
            return ctx.enter_context(nc.sbuf_tensor(name, shape, dt))

        PW = UW + E
        ones = sb("ones", [P, P], F32)
        ones_bf = sb("ones_bf", [P, P], BF16)
        ones_r = sb("ones_r", [1, P], F32R)
        before = sb("before", [P, P], BF16)
        first_key = sb("first_key", [P, E], F32)
        region = sb("region", [P, E], F32)
        keep_sum = sb("keep_sum", [P, E, GT + 1], F32)
        half_power = sb("half_power", [P, GT], F32)
        steps = sb("steps", [1, J], F32)
        dest = sb("dest", [P, K * GT], F32)
        pad_row = sb("pad_row", [P, ROW], F32)

        proj_hi = sb("proj_hi", [P, PW], F32R)
        proj_lo = sb("proj_lo", [P, PW], F32R)
        gate_hi = sb("gate_hi", [P, D], F32R)
        gate_lo = sb("gate_lo", [P, D], F32R)
        gbias_raw = sb("gbias_raw", [1, D], F32)
        gbias_hi = sb("gbias_hi", [1, D], F32R)
        gbias_lo = sb("gbias_lo", [1, D], F32R)
        mix_hi = sb("mix_hi", [P, SC * 4 * P], F32R)
        mix_lo = sb("mix_lo", [P, SC * 4 * P], F32R)
        h_bias = sb("h_bias", [P, 2, D], F32)
        g_bias = sb("g_bias", [P, E], F32)

        ew_raw = sb("ew_raw", [P, 2, EW], F32)
        mix_raw = ew_raw[:, 0, 0:SC * 4 * P]
        proj_raw, gate_raw = ew_raw[:, 1, 0:PW], ew_raw[:, 1, PW:PW + D]
        sums = ew_raw[0:2, 1, PW + D:PW + D + SC * S]
        pbias = ew_raw[0:2, 1, PW + D + SC * S:PW + 2 * D + SC * S]
        x_in_sb = sb("x_in_sb", [P, 2, GT, D], F32)
        xn = sb("xn", [P, 2, GT, D], F32)
        stats = sb("stats", [P, GT, 6], F32)
        moments = sb("moments", [P, GT, 2], F32)
        var_eps = sb("var_eps", [P, GT], F32)
        rstd = sb("rstd", [P, GT], F32)
        xt_hi = sb("xt_hi", [P, 2, HT4 * P], F32R)
        xt_lo = sb("xt_lo", [P, 2, HT4 * P], F32R)
        u_hi = sb("u_hi", [P, GT, UW], F32R)
        u_lo = sb("u_lo", [P, GT, UW], F32R)
        h = sb("h", [P, GT, D], F32)
        ht_hi, ht_lo = xt_hi, xt_lo
        rows = sb("rows", [P, 2, K * GT, ROW], F32)
        slot_row = sb("slot_row", [P, 2, K * GT], U32)

        logits = sb("logits", [P, GT, E], F32)
        logits2 = sb("logits2", [P, GT, E], F32)
        key = sb("key", [P, 2, GT, E], F32)
        chosen = sb("chosen", [P, K, GT, E], F32)
        best = sb("best", [P, K, GT], F32)
        best_key = sb("best_key", [P, K, GT], F32)
        gap = sb("gap", [P, GT], F32)
        ratio = sb("ratio", [P, GT], F32)
        denom = sb("denom", [P, GT], F32)
        weight = sb("weight", [P, K, GT], F32)
        mask = sb("mask", [P, E, GT + 1], BF16)
        prefix = sb("prefix", [P, E, GT + 1], BF16)
        position = sb("position", [P, E, GT], F32)
        picked = sb("picked", [P, K, GT, E], F32)

        count = sb("count", [1, E], F32)
        padded = sb("padded", [1, E], I32)
        tiles_i = sb("tiles_i", [1, E], I32)
        tiles_f = sb("tiles_f", [1, E], F32)
        tile_end = sb("tile_end", [1, E], F32)
        jump = sb("jump", [1, E], F32)
        passed, jumped = (ew_raw[0:1, j, 0:J * E].rearrange("p (j e) -> p j e", e=E) for j in range(2))
        plan_f = sb("plan_f", [1, 2, J], F32)
        plan_g = sb("plan_g", [1, J], F32)
        tail_f = sb("tail_f", [1, E], F32)

        xt_bank, u_bank, h_bank = banks[0:2], banks[2:4], banks[4:6]
        pos_bank, gate_bank = banks[6], banks[7]

        consts_in, mix_in = sem("consts_in"), sem("mix_in")
        filled, filled2, made = sem("filled"), sem("filled2"), sem("made")
        split_hi, split_lo = sem("split_hi"), sem("split_lo")
        mix_hi_done, mix_lo_done = sem("mix_hi_done"), sem("mix_lo_done")
        hb_ready, hb_done = sem("hb_ready"), sem("hb_done")
        gb_ready, gb_done = sem("gb_ready"), sem("gb_done")
        x_in = [sem(f"x_in{k}") for k in range(2)]
        w_in = [sem(f"w_in{k}") for k in range(2)]
        xn_out = [sem(f"xn_out{k}") for k in range(2)]
        rows_free = sem("rows_free")
        sent = [sem(f"sent{k}") for k in range(2)]
        stats_seen = sem("stats_seen")
        stats_done, moments_done, var_done = sem("stats_done"), sem("moments_done"), sem("var_done")
        rstd_done, xn_done = sem("rstd_done"), sem("xn_done")
        xt_ready, xt_hi_done, xt_lo_done = sem("xt_ready"), sem("xt_hi_done"), sem("xt_lo_done")
        xt_free = sem("xt_free")
        u_ready, u_hi_done, u_free = sem("u_ready"), sem("u_hi_done"), sem("u_free")
        logits_done = sem("logits_done")
        h_ready, h_free = sem("h_ready"), sem("h_free")
        ht_ready, ht_hi_done = sem("ht_ready"), sem("ht_hi_done")
        gate_ready, gate_free, tanh_done = sem("gate_ready"), sem("gate_free"), sem("tanh_done")
        route = sem("route")
        gap_done, exp_done, weight_done = sem("gap_done"), sem("exp_done"), sem("weight_done")
        prefix_done, pos_ready = sem("prefix_done"), sem("pos_ready")
        idx_done, dest_done = sem("idx_done"), sem("dest_done")
        row0_done, row1_done = sem("row0_done"), sem("row1_done")
        w_hi_done, w_lo_done = sem("w_hi_done"), sem("w_lo_done")
        count_ready, planning, planned = sem("count_ready"), sem("planning"), sem("planned")
        pad_out = sem("pad_out")

        block = ctx.enter_context(nc.Block())

        def groups(eng, body):
            for q in range(NG):
                body(q, q // 2, q % 2)

        @block.sync
        def _(sp):
            for n, w in enumerate(w_proj):
                sp.dma_start(proj_raw[:, n * DP:(n + 1) * DP], w).then_inc(consts_in, 16)
            sp.dma_start(proj_raw[:, UW:PW], w_g).then_inc(consts_in, 16)

            def body(q, r, k):
                sp.dma_start(x_in_sb[:, k], x_tiles[:, bass.ds(q * GT, GT), :]).then_inc(x_in[k], 16)
                for j in range(2):
                    e = q * 2 + j
                    sp.wait_ge(w_lo_done, q * 2 + 1)
                    if j == 0:
                        sp.wait_ge(mix_lo_done, 1)
                    else:
                        sp.wait_ge(split_lo, 3)
                        sp.wait_ge(hb_ready, 1)
                    for m, w in enumerate((w1, w3)):
                        sp.dma_start(ew_raw[:, j, m * HID:(m + 1) * HID],
                                     w[bass.ds(e, 1)].rearrange("a p h -> p (a h)")).then_inc(w_in[j], 16)
                    sp.dma_start(ew_raw[:, j, 2 * HID:EW].rearrange("p (c d) -> p c d", c=NC),
                                 w2[bass.ds(e, 1)].rearrange("a (c p) d -> p (a c) d", p=P)).then_inc(w_in[j], 16)
                    if j == 0:
                        sp.wait_ge(xn_done, q * GT + GT)
                        sp.dma_start(xn_tiles[:, bass.ds(q * GT, GT), :], xn[:, k]).then_inc(xn_out[k], 16)

            groups(sp, body)
            sp.wait_ge(filled, 1)
            sp.wait_ge(made, 5)
            sp.dma_start(rows_dram[IDLE:IDLE + P, :], pad_row[:]).then_inc(pad_out, 16)
            sp.wait_ge(planned, 3)
            for e in range(E):
                start = sp.value_load(plan[0:1, 2 * J + e:2 * J + e + 1], min_val=0, max_val=IDLE - P)
                sp.dma_start(rows_dram[bass.ds(start, P), :], pad_row[:]).then_inc(pad_out, 16)
            sp.wait_ge(pad_out, 16 * (E + 1))
            for k in range(2):
                sp.wait_ge(xn_out[k], 16 * (NG // 2) + 16)

        @block.gpsimd
        def _(pool):
            pool.memset(pad_row[:], 0.0).then_inc(filled, 1)
            pool.memset(half_power[:], -0.5).then_inc(filled, 1)
            pool.memset(ones[:], 1.0).then_inc(filled, 1)
            pool.memset(ones_bf[:], 1.0).then_inc(filled, 1)
            pool.memset(keep_sum[:], 1.0).then_inc(filled, 1)
            pool.memset(mask[:], 0.0).then_inc(filled, 1)
            pool.wait_ge(filled, 6)
            pool.affine_select(out=ident[:], in_=ones[:], compare_op=ALU.is_equal, fill=0.0, base=0,
                               pattern=[[-1, P]], channel_multiplier=1).then_inc(made, 1)
            pool.affine_select(out=before[:], in_=ones_bf[:], compare_op=ALU.is_gt, fill=0.0, base=0,
                               pattern=[[1, P]], channel_multiplier=-1).then_inc(made, 1)
            pool.iota(first_key[:], [[-1, E]], base=E, channel_multiplier=0,
                      allow_small_or_imprecise_dtypes=True).then_inc(made, 1)
            pool.iota(region[:], [[REG, E]], base=0, channel_multiplier=0,
                      allow_small_or_imprecise_dtypes=True).then_inc(made, 1)
            pool.iota(pad_row[:, D:ROW].bitcast(U32), [[0, 1]], base=DUMP, channel_multiplier=1).then_inc(made, 1)
            pool.iota(dest[:], [[TOK, K], [P, GT]], base=0, channel_multiplier=1,
                      allow_small_or_imprecise_dtypes=True).then_inc(made, 1)
            pool.iota(steps[:], [[1, J]], base=0, channel_multiplier=0,
                      allow_small_or_imprecise_dtypes=True).then_inc(made, 1)
            pool.memset(keep_sum[:, :, 0:1], 0.0).then_inc(made, 1)

            def inverse_deviation(q):
                pool.wait_ge(var_done, q + 1)
                pool.wait_ge(xn_done, q * GT)
                pool.tensor_tensor(rstd[:], var_eps[:], half_power[:], ALU.pow).then_inc(rstd_done, 1)

            inverse_deviation(0)
            for q in range(NG):
                k = q % 2
                pool.wait_ge(idx_done, q + 2)
                pool.wait_ge(dest_done, q + 1)
                for n in range(K * GT):
                    i, slot = n // K, n % K
                    pool.wait_ge(row1_done if slot else row0_done, q * GT + i + 1 + slot)
                    at = slot * GT + i
                    pool.indirect_dma_start(
                        out=rows_dram[:, :],
                        out_offset=bass.IndirectOffsetOnAxis(ap=slot_row[:, k, at:at + 1], axis=0),
                        in_=rows[:, k, at, :], in_offset=None).then_inc(sent[k], 16)
                    if n == 3 and q:
                        pool.wait_ge(sent[1 - k], 16 * K * GT * ((q + 1) // 2))
                        pool.sem_inc(rows_free, 1)
                    if n == 10 and q + 1 < NG:
                        inverse_deviation(q + 1)
            for k in range(2):
                pool.wait_ge(sent[k], 16 * K * GT * (NG // 2))

        @block.scalar
        def _(act):
            act.dma_start(gate_raw, w_gate).then_inc(consts_in, 16)
            act.dma_start(gbias_raw[:], b_gate.unsqueeze(0)).then_inc(consts_in, 16)
            act.dma_start(g_bias[:], b_g.partition_broadcast(P)).then_inc(consts_in, 16)
            act.dma_start(sums, mix_sums).then_inc(consts_in, 16)
            for n, b in enumerate(b_proj):
                act.dma_start(pbias[n % 2:n % 2 + 1, (n // 2) * DP:(n // 2 + 1) * DP],
                              b.unsqueeze(0)).then_inc(consts_in, 16)
            act.dma_start(mix_raw, mix).then_inc(mix_in, 16)
            act.preload_act_table(ACT.Exp)
            act.wait_ge(consts_in, 16 * 13)
            act.activation(proj_hi[:], proj_raw, ACT.Copy).then_inc(split_hi, 1)
            act.activation(gate_hi[:], gate_raw, ACT.Copy).then_inc(split_hi, 1)
            act.activation(gbias_hi[:], gbias_raw[:], ACT.Copy).then_inc(split_hi, 1)
            act.wait_ge(filled, 6)
            act.activation(ones_r[:], ones[0:1, :], ACT.Copy).then_inc(split_hi, 1)
            act.wait_ge(mix_in, 16)
            act.activation(mix_hi[:], mix_raw, ACT.Copy).then_inc(mix_hi_done, 1)

            def body(q, r, k):
                for half in range(2):
                    act.wait_ge(xt_ready, q * 2 + half + 1)
                    act.activation(xt_hi[:, half], xt_bank[half][:], ACT.Copy).then_inc(xt_hi_done, 1)
                for i in range(GT):
                    act.wait_ge(u_ready, q * GT + i + 1)
                    act.activation(u_hi[:, i], u_bank[i % 2][:, 0:UW], ACT.Copy).then_inc(u_hi_done, 1)
                act.wait_ge(gap_done, q + 1)
                act.activation(ratio[:], gap[:], ACT.Exp).then_inc(exp_done, 1)
                act.wait_ge(weight_done, q * 2 + 2)
                act.wait_ge(rows_free, q + 1)
                for i in range(GT):
                    act.activation(rows[:, k, GT + i, 0:D], xn[:, k, i], ACT.Copy,
                                   scale=weight[:, 1, i:i + 1]).then_inc(row1_done, 1)
                for half in range(2):
                    act.wait_ge(ht_ready, q * 2 + half + 1)
                    act.activation(ht_hi[:, half], xt_bank[half][:], ACT.Copy).then_inc(ht_hi_done, 1)
                for j in range(2):
                    act.wait_ge(w_in[j], q * 48 + 48)
                    e = q * 2 + j
                    act.activation(ew[:, e * EC:(e + 1) * EC, 0], ew_raw[:, j].rearrange("p (c d) -> p c d", c=EC),
                                   ACT.Copy).then_inc(w_hi_done, 1)
                for half in range(2):
                    act.wait_ge(gate_ready, q * 2 + half + 1)
                    act.activation(gate_bank[:], gate_bank[:], ACT.Tanh, scale=0.5).then_inc(tanh_done, 1)

            groups(act, body)

        @block.vector
        def _(dve):
            dve.wait_ge(split_hi, 3)
            dve.tensor_tensor(proj_lo[:], proj_raw, proj_hi[:].bitcast(F32), ALU.subtract).then_inc(split_lo, 1)
            dve.tensor_tensor(gate_lo[:], gate_raw, gate_hi[:].bitcast(F32), ALU.subtract).then_inc(split_lo, 1)
            dve.tensor_tensor(gbias_lo[:], gbias_raw[:], gbias_hi[:].bitcast(F32), ALU.subtract
                              ).then_inc(split_lo, 1)
            dve.wait_ge(made, 8)

            for k in range(2):
                dve.sem_inc(xn_out[k], 16)
            dve.sem_inc(rows_free, 2)
            dve.sem_inc(exp_done, 1)
            dve.sem_inc(row1_done, 1)
            dve.sem_inc(w_lo_done, 1)
            NR = 17

            def body(q, r, k):
                done = [0]

                def chain(ins):
                    ins.then_inc(route, 1)
                    done[0] += 1
                    dve.wait_ge(route, q * NR + done[0])

                dve.wait_ge(x_in[k], r * 16 + 16)
                for i in range(GT):
                    dve.bn_stats(stats[:, i], x_in_sb[:, k, i]).then_inc(stats_done, 1)
                dve.wait_ge(stats_done, q * GT + GT)
                dve.sem_inc(stats_seen, 1)
                for i in range(GT):
                    dve.bn_aggr(moments[:, i], stats[:, i]).then_inc(moments_done, 1)
                dve.wait_ge(moments_done, q * GT + GT)
                dve.tensor_scalar(var_eps[:], moments[:, :, 1], EPS, None, ALU.add).then_inc(var_done, 1)
                dve.wait_ge(rstd_done, q + 1)
                dve.wait_ge(xn_out[k], r * 16 + 16)
                for i in range(GT):
                    dve.tensor_scalar(xn[:, k, i], x_in_sb[:, k, i], moments[:, i, 0:1], rstd[:, i:i + 1],
                                      ALU.subtract, ALU.mult).then_inc(xn_done, 1)
                for half in range(2):
                    dve.wait_ge(xt_hi_done, q * 2 + half + 1)
                    dve.tensor_tensor(xt_lo[:, half], xt_bank[half][:], xt_hi[:, half].bitcast(F32),
                                      ALU.subtract).then_inc(xt_lo_done, 1)
                for i in range(GT):
                    dve.wait_ge(u_hi_done, q * GT + i + 1)
                    dve.tensor_tensor(logits[:, i], u_bank[i % 2][:, UW:PW], g_bias[:], ALU.add
                                      ).then_inc(logits_done, 1)
                    dve.tensor_tensor(u_lo[:, i], u_bank[i % 2][:, 0:UW], u_hi[:, i].bitcast(F32),
                                      ALU.subtract).then_inc(u_free, 1)
                dve.wait_ge(logits_done, q * GT + GT)
                for s, l in enumerate((logits, logits2)):
                    chain(dve.tensor_reduce(best[:, s], l[:], X, ALU.max))
                    chain(dve.tensor_tensor(key[:, 0], l[:], best[:, s].unsqueeze(2).broadcast_to([P, GT, E]),
                                            ALU.is_equal))
                    chain(dve.tensor_tensor(key[:, 1], key[:, 0],
                                            first_key[:].unsqueeze(1).broadcast_to([P, GT, E]), ALU.mult))
                    chain(dve.tensor_reduce(best_key[:, s], key[:, 1], X, ALU.max))
                    chain(dve.tensor_tensor(chosen[:, s], key[:, 1],
                                            best_key[:, s].unsqueeze(2).broadcast_to([P, GT, E]), ALU.is_equal))
                    if s == 0:
                        chain(dve.scalar_tensor_tensor(out=logits2[:], in0=chosen[:, 0], scalar=LOWEST,
                                                       in1=logits[:], op0=ALU.mult, op1=ALU.add))
                        dve.wait_ge(exp_done, q + 1)
                dve.tensor_tensor(gap[:], best[:, 1], best[:, 0], ALU.subtract).then_inc(gap_done, 1)
                chain(dve.tensor_tensor(mask[:, :, 1:GT + 1], chosen[:, 0].rearrange("p i e -> p e i"),
                                        chosen[:, 1].rearrange("p i e -> p e i"), ALU.add))
                dve.tensor_tensor_scan(prefix[:].rearrange("p e i -> p (e i)"),
                                       keep_sum[:].rearrange("p e i -> p (e i)"),
                                       mask[:].rearrange("p e i -> p (e i)"), 0.0, ALU.mult, ALU.add
                                       ).then_inc(prefix_done, 1)
                dve.wait_ge(exp_done, q + 2)
                chain(dve.tensor_scalar(denom[:], ratio[:], 1.0, None, ALU.add))
                dve.wait_ge(row1_done, q * GT + 1)
                dve.reciprocal(weight[:, 0], denom[:]).then_inc(weight_done, 1)
                dve.wait_ge(weight_done, q * 2 + 1)
                dve.tensor_tensor(weight[:, 1], ratio[:], weight[:, 0], ALU.mult).then_inc(weight_done, 1)
                dve.wait_ge(rows_free, q + 1)
                for i in range(GT):
                    dve.tensor_scalar(rows[:, k, i, 0:D], xn[:, k, i], weight[:, 0, i:i + 1], None,
                                      ALU.mult).then_inc(row0_done, 1)
                chain(dve.tensor_copy(rows[:, k, :, D].bitcast(U32), dest[:]))
                dve.tensor_scalar(dest[:], dest[:], float(GT * P), None, ALU.add).then_inc(dest_done, 1)
                dve.wait_ge(pos_ready, q + 1)
                chain(dve.tensor_tensor(position[:], pos_bank[:, 0:E * GT].rearrange("p (e i) -> p e i", e=E),
                                        region[:].unsqueeze(2).broadcast_to([P, E, GT]), ALU.add))
                chain(dve.tensor_tensor(picked[:], chosen[:],
                                        position[:].rearrange("p e i -> p i e").unsqueeze(1)
                                        .broadcast_to([P, K, GT, E]), ALU.mult))
                with nc.allow_low_precision(reason="a whole number below 2^24, summed in float32"):
                    dve.tensor_reduce(slot_row[:, k], picked[:].rearrange("p s i e -> p (s i) e"), X, ALU.add
                                      ).then_inc(idx_done, 1)
                chain(dve.tensor_copy(mask[:, :, 0], prefix[:, :, GT]))
                assert done[0] == NR, done[0]

                for tb in range(2):
                    dve.wait_ge(h_ready, q * 2 + tb + 1)
                    if tb == 0:
                        dve.wait_ge(hb_done, 2)
                    dve.tensor_tensor(h[:].rearrange("p (b t) d -> p t b d", t=2)[:, tb],
                                      h_bank[tb][:].rearrange("p (b d) -> p b d", b=GB),
                                      h_bias[:, tb].unsqueeze(1).broadcast_to([P, GB, D]), ALU.add
                                      ).then_inc(h_free, 1)
                for half in range(2):
                    dve.wait_ge(ht_hi_done, q * 2 + half + 1)
                    dve.tensor_tensor(ht_lo[:, half], xt_bank[half][:], ht_hi[:, half].bitcast(F32),
                                      ALU.subtract).then_inc(xt_free, 1)
                for j in range(2):
                    dve.wait_ge(w_hi_done, q * 2 + j + 1)
                    e = q * 2 + j
                    dve.tensor_tensor(ew[:, e * EC:(e + 1) * EC, 1], ew_raw[:, j].rearrange("p (c d) -> p c d", c=EC),
                                      ew[:, e * EC:(e + 1) * EC, 0].bitcast(F32), ALU.subtract
                                      ).then_inc(w_lo_done, 1)
                for half in range(2):
                    dve.wait_ge(tanh_done, q * 2 + half + 1)
                    dve.scalar_tensor_tensor(
                        out=gated[:, bass.ds(q * GT + half * HT4, HT4), :].rearrange("p i d -> p (i d)"),
                        in0=gate_bank[:], scalar=1.0,
                        in1=h[:, half * HT4:(half + 1) * HT4].rearrange("p i d -> p (i d)"),
                        op0=ALU.add, op1=ALU.mult).then_inc(gate_free, 1)

            dve.wait_ge(mix_hi_done, 1)
            dve.tensor_tensor(mix_lo[:], mix_raw, mix_hi[:].bitcast(F32), ALU.subtract).then_inc(mix_lo_done, 1)
            dve.wait_ge(hb_ready, 1)
            dve.tensor_copy(h_bias[:].rearrange("p t d -> p (t d)"), gate_bank[:, 0:2 * D]).then_inc(hb_done, 2)
            groups(dve, body)

            done = [0]

            def then(ins):
                ins.then_inc(planning, 1)
                done[0] += 1
                dve.wait_ge(planning, done[0])

            dve.wait_ge(count_ready, 1)
            then(dve.tensor_copy(count[:], pos_bank[0:1, 0:E]))
            then(dve.tensor_scalar(padded[:], count[:], float(P - 1), None, ALU.add))
            then(dve.tensor_scalar(tiles_i[:], padded[:], 7, None, ALU.arith_shift_right))
            then(dve.tensor_copy(tiles_f[:], tiles_i[:]))
            then(dve.tensor_tensor_scan(tile_end[:], ones[0:1, 0:E], tiles_f[:], 0.0, ALU.mult, ALU.add))
            then(dve.tensor_scalar(jump[:], tiles_f[:], float(-P), float(REG), ALU.mult, ALU.add))
            then(dve.tensor_tensor(passed, steps[:].unsqueeze(2).broadcast_to([1, J, E]),
                                   tile_end[:].unsqueeze(1).broadcast_to([1, J, E]), ALU.is_ge))
            then(dve.tensor_tensor(jumped, passed, jump[:].unsqueeze(1).broadcast_to([1, J, E]),
                                   ALU.mult))
            then(dve.tensor_reduce(plan_f[:, 0], jumped, X, ALU.add))
            then(dve.tensor_reduce(plan_f[:, 1], passed, X, ALU.add))
            then(dve.scalar_tensor_tensor(out=plan_g[:], in0=steps[:], scalar=float(P), in1=plan_f[:, 0],
                                          op0=ALU.mult, op1=ALU.add))
            dve.tensor_scalar(plan[:, 0:J], plan_g[:], float(IDLE), None, ALU.min).then_inc(planned, 1)
            dve.tensor_scalar(plan[:, J:2 * J], plan_f[:, 1], float(E - 1), float(2 * EW), ALU.min, ALU.mult
                              ).then_inc(planned, 1)
            dve.tensor_tensor(plan[:, 2 * J:], count[:], region[0:1, :], ALU.add).then_inc(planned, 1)

        @block.tensor
        def _(pe):
            def product(to, lhs, rhs, first=True, last=True):
                (a_hi, a_lo), (b_hi, b_lo) = lhs, rhs
                pe.matmul(to, a_hi, b_hi, start=first, stop=False, skip_group_check=True)
                pe.matmul(to, a_hi, b_lo, start=False, stop=False, skip_group_check=True)
                return pe.matmul(to, a_lo, b_hi, start=False, stop=last, skip_group_check=True)

            pe.wait_ge(made, 1)
            pe.sem_inc(xt_free, 2)
            pe.sem_inc(u_free, 2)
            pe.sem_inc(gate_free, 1)
            pe.sem_inc(h_free, 2)
            pe.sem_inc(idx_done, 1)

            def mixing(q, tb):
                pe.wait_ge(h_free, q * 2 + 2)
                halves = [(0, 1), (1, 0)] if tb else [(0, 0)]
                for i in range(SC):
                    to = h_bank[tb][:].rearrange("p (b s c) -> p b s c", b=GB, s=SC)[:, :, i]
                    terms = [(src, blk, part) for src, blk in halves for part in range(2)]
                    for n, (src, blk, part) in enumerate(terms):
                        at = ((i * 2 + part) * 2 + blk) * P
                        col = (i * 2 + part) * DP
                        u = [t[:].rearrange("p (b t) c -> p t b c", t=2)[:, src, :, col:col + DP]
                             for t in (u_hi, u_lo)]
                        mm = product(to, (mix_hi[:, at:at + P], mix_lo[:, at:at + P]), u,
                                     n == 0, n == len(terms) - 1)
                mm.then_inc(h_ready, 1)

            def body(q, r, k):
                for half in range(2):
                    pe.wait_ge(xn_done, q * GT + (half + 1) * HT4)
                    pe.wait_ge(xt_free, q * 2 + half + 1)
                    for i in range(HT4):
                        t = pe.transpose(xt_bank[half][:, i * P:(i + 1) * P], xn[:, k, half * HT4 + i], ident[:])
                    t.then_inc(xt_ready, 1)
                for i in range(GT):
                    half, at = i // HT4, (i % HT4) * P
                    pe.wait_ge(xt_lo_done, q * 2 + half + 1)
                    pe.wait_ge(u_free, q * GT + i + 1)
                    product(u_bank[i % 2][:, 0:PW], (xt_hi[:, half, at:at + P], xt_lo[:, half, at:at + P]),
                            (proj_hi[:], proj_lo[:])).then_inc(u_ready, 1)
                pe.wait_ge(u_free, q * GT + GT + 2)
                if k == 0:
                    pe.wait_ge(mix_lo_done, 1)
                mixing(q, 0)
                pe.wait_ge(prefix_done, q + 1)
                pe.wait_ge(idx_done, q + 1)
                to = pos_bank[:, 0:E * GT].rearrange("p (e i) -> p e i", e=E)
                pe.matmul(to, before[:], mask[:, :, 1:GT + 1], start=True, stop=False)
                pe.matmul(to, ones_bf[:], prefix[:, :, 0:GT], start=False, stop=True).then_inc(pos_ready, 1)
                mixing(q, 1)
                for half in range(2):
                    pe.wait_ge(h_free, q * 2 + 4)
                    for i in range(HT4):
                        t = pe.transpose(xt_bank[half][:, i * P:(i + 1) * P], h[:, half * HT4 + i], ident[:])
                    t.then_inc(ht_ready, 1)
                for half in range(2):
                    pe.wait_ge(xt_free, q * 2 + half + 3)
                    pe.wait_ge(gate_free, q * 2 + half + 1)
                    to = gate_bank[:].rearrange("p (i d) -> p i d", i=HT4)
                    for n, b in enumerate((gbias_hi, gbias_lo)):
                        pe.matmul(to, ones_r[:], b[:].unsqueeze(1).broadcast_to([1, HT4, D]),
                                  start=(n == 0), stop=False, skip_group_check=True)
                    for i in range(HT4):
                        at = i * P
                        mm = product(gate_bank[:, i * D:(i + 1) * D],
                                     (ht_hi[:, half, at:at + P], ht_lo[:, half, at:at + P]),
                                     (gate_hi[:], gate_lo[:]), False, i == HT4 - 1)
                    mm.then_inc(gate_ready, 1)

            pe.wait_ge(consts_in, 16 * 13)
            for tb in range(2):
                for i in range(SC):
                    mm = pe.matmul(gate_bank[:, tb * D + i * DP:tb * D + (i + 1) * DP],
                                   sums[:, i * S + tb * P:i * S + (tb + 1) * P],
                                   pbias[:, i * DP:(i + 1) * DP], start=True, stop=True)
            mm.then_inc(hb_ready, 1)
            pe.wait_ge(hb_done, 2)
            pe.wait_ge(split_lo, 3)
            pe.wait_ge(split_hi, 4)
            pe.wait_ge(made, 8)
            groups(pe, body)
            pe.wait_ge(route, NG * 17)
            pe.wait_ge(idx_done, NG + 1)
            pe.matmul(pos_bank[:, 0:E], ones_bf[:], mask[:, :, 0], start=True, stop=True).then_inc(count_ready, 1)


def experts(nc, sem, banks, ident, ew, plan, rows_dram, y_dram, x_tiles, xn_tiles,
            x_all, xn_all, tail_in):
    ctx = ExitStack()
    with ctx:
        def sb(name, shape, dt):
            return ctx.enter_context(nc.sbuf_tensor(name, shape, dt))

        row = sb("row", [P, TURN, ROW], F32)
        xt_hi = sb("row_t_hi", [P, 2, P], F32R)
        xt_lo = sb("row_t_lo", [P, 2, P], F32R)
        silu = sb("silu_a", [P, 2, HID], F32)
        hid = sb("hid", [P, 2, HID], F32)
        ht_hi = sb("hid_t_hi", [P, 2, HID], F32R)
        ht_lo = sb("hid_t_lo", [P, 2, HID], F32R)
        y = sb("y", [P, TURN, D], F32)

        a_bank, c_bank, ht_bank = banks[0:2], banks[2:4], banks[4:6]
        xt_bank, y_bank = banks[6], banks[7]

        row_in = [sem(f"row_in{k}") for k in range(TURN)]
        y_out = [sem(f"y_out{k}") for k in range(TURN)]
        xt_ready, xt_hi_done, xt_lo_done = sem("e_xt_ready"), sem("e_xt_hi_done"), sem("e_xt_lo_done")
        a_ready, silu_done = sem("a_ready"), sem("silu_done")
        c_ready, hid_done = sem("c_ready"), sem("hid_done")
        ht_ready, ht_hi_done, ht_lo_done = sem("e_ht_ready"), sem("e_ht_hi_done"), sem("e_ht_lo_done")
        y_ready, y_done, y_seen = sem("y_ready"), sem("y_done"), sem("y_seen")

        block = ctx.enter_context(nc.Block())

        def tiles(eng, turn, head=1):
            for g in range(head):
                turn(g)
            with eng.Fori(head, TURNS - 1) as g:
                turn(g)
            turn(TURNS - 1)

        def has(j, back):
            return not isinstance(j, int) or 0 <= j - back < J

        def loaded(eng, first, count, most):
            return nc.values_load_multi_w_load_instructions(
                plan[0:1, bass.ds(first, count)], engines=[eng], min_val=0, max_val=most,
                skip_runtime_bounds_check_because="the plan is clamped to this range on the chip")[1]

        @block.sync
        def _(sp):
            def turn(g):
                starts = loaded(mybir.EngineType.SP, g * TURN, TURN, IDLE)
                for k in range(TURN):
                    if not isinstance(g, int) or g:
                        sp.wait_ge(y_out[k], g * 16)
                    sp.dma_start(row[:, k], rows_dram[bass.ds(starts[k], P), :]).then_inc(row_in[k], 16)
                    if k == TURN // 2 and (not isinstance(g, int) or g):
                        part = bass.ds(g * PART - PART, PART)
                        sp.dma_start(x_all[:, part, :], x_tiles[:, part, :]).then_inc(tail_in, 16)
                        sp.dma_start(xn_all[:, part, :], xn_tiles[:, part, :]).then_inc(tail_in, 16)

            tiles(sp, turn)

        @block.gpsimd
        def _(pool):
            with pool.Fori(0, TURNS) as g:
                for k in range(TURN):
                    pool.wait_ge(y_done, g * TURN + k + 1)
                    pool.sem_inc(y_seen, 1)
                    pool.indirect_dma_start(
                        out=y_dram[:, :],
                        out_offset=bass.IndirectOffsetOnAxis(ap=row[:, k, D:ROW].bitcast(U32), axis=0),
                        in_=y[:, k], in_offset=None,
                        bounds_check=DUMP - 1, oob_is_err=False).then_inc(y_out[k], 16)
            for k in range(TURN):
                pool.wait_ge(y_out[k], 16 * TURNS)

        @block.scalar
        def _(act):
            act.preload_act_table(ACT.Silu)
            act.sem_inc(a_ready, 1)
            act.sem_inc(ht_ready, 2)

            def row_hi(j):
                act.wait_ge(xt_ready, j + 2)
                b = (k_of[0] + 1) % 2
                act.activation(xt_hi[:, b], xt_bank[:, 0:P], ACT.Copy).then_inc(xt_hi_done, 1)

            def hidden_hi(j):
                act.wait_ge(ht_ready, j + 2)
                b = (k_of[0] - 1) % 2
                act.activation(ht_hi[:, b], ht_bank[b][:], ACT.Copy).then_inc(ht_hi_done, 1)

            k_of = [-1]

            def turn(g):
                for k in range(TURN):
                    j = g * TURN + k
                    k_of[0] = k
                    if has(j, -1):
                        row_hi(j)
                    act.wait_ge(a_ready, j + 2)
                    act.activation(silu[:, k % 2], a_bank[k % 2][:], ACT.Silu).then_inc(silu_done, 1)
                    if has(j, 1):
                        hidden_hi(j)

            row_hi(-1)
            tiles(act, turn)
            k_of[0] = TURN
            hidden_hi(J)

        @block.vector
        def _(dve):
            dve.sem_inc(silu_done, 1)
            dve.sem_inc(c_ready, 1)
            dve.sem_inc(ht_hi_done, 2)
            dve.sem_inc(y_ready, 3)

            def row_lo(j, b):
                dve.wait_ge(xt_hi_done, j + 2)
                dve.tensor_tensor(xt_lo[:, b], xt_bank[:, 0:P], xt_hi[:, b].bitcast(F32), ALU.subtract
                                  ).then_inc(xt_lo_done, 1)

            def hidden_lo(j, b):
                dve.wait_ge(ht_hi_done, j + 2)
                dve.tensor_tensor(ht_lo[:, b], ht_bank[b][:], ht_hi[:, b].bitcast(F32), ALU.subtract
                                  ).then_inc(ht_lo_done, 1)

            def result(j, g, k):
                dve.wait_ge(y_ready, j + 2)
                if not isinstance(g, int) or g:
                    dve.wait_ge(y_out[k], g * 16)
                dve.tensor_reduce(y[:, k], y_bank[:, 0:2 * D].rearrange("p (a d) -> p d a", a=2), X, ALU.add
                                  ).then_inc(y_done, 1)

            def turn(g):
                for k in range(TURN):
                    j = g * TURN + k
                    if has(j, -1):
                        row_lo(j, (k + 1) % 2)
                    dve.wait_ge(silu_done, j + 2)
                    dve.wait_ge(c_ready, j + 2)
                    dve.tensor_tensor(hid[:, k % 2], c_bank[k % 2][:], silu[:, k % 2], ALU.mult
                                      ).then_inc(hid_done, 1)
                    if has(j, 2):
                        result(j, g if k >= 2 else g - 1, (k - 2) % TURN)
                    if has(j, 1):
                        hidden_lo(j, (k - 1) % 2)

            row_lo(-1, 0)
            tiles(dve, turn, head=2)
            result(J, TURNS - 1, TURN - 2)
            hidden_lo(J, (J - 1) % 2)
            result(J + 1, TURNS - 1, TURN - 1)

        @block.tensor
        def _(pe):
            pe.sem_inc(hid_done, 1)
            pe.sem_inc(ht_lo_done, 2)

            def transpose_row(g, k):
                pe.wait_ge(row_in[k], g * 16 + 16)
                pe.transpose(xt_bank[:, 0:P], row[:, k, 0:D], ident[:]).then_inc(xt_ready, 1)

            def chunk(col, c, part, n=1):
                at = bass.ds(col + (2 * c + part) * P, (2 * n - 1) * P) if n > 1 else None
                if n > 1:
                    w = flat[:, bass.ds(col + 2 * c * P + part * P, 2 * n * P)] if part == 0 else \
                        flat[:, bass.ds(col + 2 * c * P, 2 * n * P)]
                    return w.rearrange("p (c s d) -> p c s d", s=2, d=P)[:, :, part]
                return flat[:, bass.ds(col + 2 * c * P, 2 * P)]

            flat = ew[:].rearrange("p c s d -> p (c s d)")

            def up(b, col):
                for c, bank, ready in ((0, a_bank[b], a_ready), (NC, c_bank[b], c_ready)):
                    hi, lo = (chunk(col, c, part, NC) for part in range(2))
                    to = bank[:].rearrange("p (c d) -> p c d", c=NC)
                    pe.matmul(to, xt_hi[:, b], hi, start=True, stop=False)
                    pe.matmul(to, xt_lo[:, b], hi, start=False, stop=False)
                    pe.matmul(to, xt_hi[:, b], lo, start=False, stop=True).then_inc(ready, 1)

            def transpose_hidden(j, b):
                pe.wait_ge(hid_done, j + 1)
                for c in range(NC):
                    t = pe.transpose(ht_bank[b][:, c * P:(c + 1) * P], hid[:, b, c * P:(c + 1) * P], ident[:])
                t.then_inc(ht_ready, 1)

            def down(j, b, col):
                pe.wait_ge(ht_lo_done, j + 1)
                for c in range(NC):
                    w = chunk(col, 2 * NC + c, 0)
                    hi, lo = ht_hi[:, b, c * P:(c + 1) * P], ht_lo[:, b, c * P:(c + 1) * P]
                    pe.matmul(y_bank[:, 0:2 * D], hi, w, start=(c == 0), stop=False, skip_group_check=True)
                    mm = pe.matmul(y_bank[:, 0:D], lo, w[:, 0:D], start=False, stop=(c == NC - 1),
                                   skip_group_check=True)
                mm.then_inc(y_ready, 1)

            def turn(g):
                lead = 2 if not isinstance(g, int) or g else 0
                columns = loaded(mybir.EngineType.PE, g * TURN + (J - lead), TURN + lead, (E - 1) * 2 * EW)
                for k in range(TURN):
                    j = g * TURN + k
                    pe.wait_ge(xt_lo_done, j + 1)
                    if has(j, -1):
                        transpose_row(g if k < TURN - 1 else g + 1, (k + 1) % TURN)
                    up(k % 2, columns[k + lead])
                    if has(j, 1):
                        transpose_hidden(j, (k - 1) % 2)
                    if has(j, 2):
                        down(j, k % 2, columns[k + lead - 2])
                return columns

            transpose_row(0, 0)
            turn(0)
            with pe.Fori(1, TURNS - 1) as g:
                turn(g)
            columns = turn(TURNS - 1)
            transpose_hidden(J, (J - 1) % 2)
            down(J, (J - 2) % 2, columns[TURN])
            down(J + 1, (J - 1) % 2, columns[TURN + 1])


def combine(nc, sem, gated, x_all, xn_all, tail_in, y_tiles, out_tiles):
    CT = 4
    ctx = ExitStack()
    with ctx:
        def sb(name, shape, dt):
            return ctx.enter_context(nc.sbuf_tensor(name, shape, dt))

        y = sb("y_pair", [P, 2, K, CT * D], F32)
        total = sb("total", [P, 2, CT * D], F32)
        ffn = sb("ffn", [P, 2, CT * D], F32)
        silu = sb("silu", [P, 2, CT * D], F32)
        res = sb("res", [P, 2, CT * D], F32)
        y_in = [sem(f"y_in{k}") for k in range(2)]
        stored = [sem(f"stored{k}") for k in range(2)]
        sum_done, ffn_done, silu_ready = sem("sum_done"), sem("ffn_done"), sem("silu_ready")
        prod_done, res_done = sem("prod_done"), sem("res_done")
        n_chunks = NT // CT
        block = ctx.enter_context(nc.Block())

        def flat(t, c):
            return t[:, bass.ds(c * CT, CT), :].rearrange("p i d -> p (i d)")

        def chunks(eng, body):
            with eng.Fori(0, n_chunks // 2) as r:
                for k in range(2):
                    body(r * 2 + k, r, k)

        @block.sync
        def _(sp):
            def body(c, r, k):
                sp.wait_ge(sum_done, r * 2 + 1)
                for s in range(K):
                    sp.dma_start(y[:, k, s].rearrange("p (i d) -> p i d", i=CT),
                                 y_tiles[:, s, bass.ds(c * CT, CT), :]).then_inc(y_in[k], 16)

            chunks(sp, body)

        @block.gpsimd
        def _(pool):
            pass

        @block.tensor
        def _(pe):
            pass

        @block.scalar
        def _(act):
            act.preload_act_table(ACT.Silu)

            def store(c, k):
                act.wait_ge(res_done, c + 1)
                act.dma_start(out_tiles[:, bass.ds(c * CT, CT), :],
                              res[:, k].rearrange("p (i d) -> p i d", i=CT)).then_inc(stored[k], 16)

            def body(c, r, k):
                act.wait_ge(ffn_done, c + 1)
                act.activation(silu[:, k], ffn[:, k], ACT.Silu).then_inc(silu_ready, 1)
                store(c, k)

            chunks(act, body)
            for k in range(2):
                act.wait_ge(stored[k], 16 * (n_chunks // 2) + 16)

        @block.vector
        def _(dve):
            dve.wait_ge(tail_in, 32 * (TURNS - 1))
            dve.sem_inc(sum_done, 1)
            dve.sem_inc(silu_ready, 1)
            for k in range(2):
                dve.sem_inc(stored[k], 16)

            def body(c, r, k):
                dve.wait_ge(y_in[k], r * 32 + 32)
                dve.tensor_tensor(total[:, k], y[:, k, 0], y[:, k, 1], ALU.add).then_inc(sum_done, 1)
                dve.wait_ge(sum_done, c + 2)
                dve.wait_ge(silu_ready, c + 1)
                dve.tensor_tensor(ffn[:, k], total[:, k], flat(xn_all, c), ALU.add).then_inc(ffn_done, 1)
                dve.wait_ge(silu_ready, c + 2)
                dve.tensor_tensor(total[:, k], silu[:, k], flat(gated, c), ALU.mult).then_inc(prod_done, 1)
                dve.wait_ge(prod_done, c + 1)
                dve.wait_ge(stored[k], r * 16 + 16)
                dve.scalar_tensor_tensor(out=res[:, k], in0=total[:, k], scalar=0.5, in1=flat(x_all, c),
                                         op0=ALU.mult, op1=ALU.add).then_inc(res_done, 1)

            chunks(dve, body)


_INS = ["L0_attn_x", "L0_attn_W_re0", "L0_attn_b_re0", "L0_attn_W_im0", "L0_attn_b_im0", "L0_attn_W_re1",
        "L0_attn_b_re1", "L0_attn_W_im1", "L0_attn_b_im1", "L0_attn_W_gate", "L0_attn_b_gate", "L0_ffn_Wg",
        "L0_ffn_bg", "L0_ffn_W1", "L0_ffn_W2", "L0_ffn_W3"]


def kernel(**inputs):
    import concourse.bacc as bacc
    from concourse.bass_utils import run_bass_kernel_spmd

    nc = bacc.Bacc("TRN2", target_bir_lowering=False, num_devices=1)
    blocks, sums = mixing_tables()
    arrays = {f"in_{name}": np.ascontiguousarray(inputs[name]) for name in _INS}
    arrays["mix_blocks"], arrays["mix_sums"] = blocks, sums
    args = [nc.dram_tensor(name, a.shape, mybir.dt.from_np(a.dtype), kind="ExternalInput").ap()
            for name, a in arrays.items()]
    args.append(nc.dram_tensor("out", (B, S, D), F32, kind="ExternalOutput").ap())
    build(nc, *args)
    r = run_bass_kernel_spmd(nc, [arrays], core_ids=[0])
    return r.results[0]["out"]
```

```python
from contextlib import ExitStack

import numpy as np

import concourse.bass as bass
import concourse.mybir as mybir

F32 = mybir.dt.float32
F32R = mybir.dt.float32r
BF16 = mybir.dt.bfloat16
I32 = mybir.dt.int32
U32 = mybir.dt.uint32
ALU = mybir.AluOpType
ACT = mybir.ActivationFunctionType
X = mybir.AxisListType.X

P = 128
B, S, D = 16, 256, 128
TOK = B * S
NT = TOK // P
E, K, HID = 8, 2, 512
NC = HID // P
SC = 2
DP = D // SC
UW = 2 * SC * DP
GT = 8
NG = NT // GT
GB = GT // 2
HT4 = GT // 2
ROW = D + 1
REG = TOK + P
IDLE = E * REG
J = K * TOK // P + E - 1
TURN = 8
TURNS = -(-J // TURN)
LAST = J - (TURNS - 1) * TURN
CT = 4
CHUNKS = NT // CT
PART = NT // (TURNS - 1)
EC = 3 * NC
EW = EC * P
DUMP = K * TOK
EPS = 1e-5
LOWEST = -3.0e38
R_VALS = np.linspace(0.999, 0.9, SC)
TH_VALS = np.linspace(0.01, 1.0, SC)


def mixing_tables():
    blocks = np.zeros((P, SC, 2, 2, P), np.float64)
    sums = np.zeros((2, SC, S), np.float64)
    lag = np.arange(P)[None, :] - np.arange(P)[:, None]
    for i in range(SC):
        a = complex(np.complex64(float(R_VALS[i]) * np.exp(1j * float(TH_VALS[i]))))
        powers = float(np.float32(1.0 - float(R_VALS[i]))) * np.exp(np.log(a) * np.arange(S))
        for part, f in enumerate((powers.real, -powers.imag)):
            blocks[:, i, part, 0] = np.where(lag >= 0, f[np.maximum(lag, 0)], 0.0)
            blocks[:, i, part, 1] = f[lag + P]
            sums[part, i] = np.cumsum(f)
    return blocks.reshape(P, -1).astype(np.float32), sums.reshape(2, -1).astype(np.float32)


def build(nc, x, w_re0, b_re0, w_im0, b_im0, w_re1, b_re1, w_im1, b_im1, w_gate, b_gate,
          w_g, b_g, w1, w2, w3, mix, mix_sums, out):
    rows_dram = nc.dram_tensor("rows_dram", (IDLE + P, ROW), F32).ap()
    y_dram = nc.dram_tensor("y_dram", (K * TOK, D), F32).ap()
    xn_dram = nc.dram_tensor("xn_dram", (TOK, D), F32).ap()

    x_tiles = x.rearrange("b (h p) d -> p (b h) d", p=P)
    out_tiles = out.rearrange("b (h p) d -> p (b h) d", p=P)
    xn_tiles = xn_dram.rearrange("(p n) d -> p n d", p=P)
    y_tiles = y_dram.rearrange("(s p n) d -> p s n d", p=P, s=K)

    ctx = ExitStack()
    with ctx:
        def keep(name, shape, dt):
            return ctx.enter_context(nc.sbuf_tensor(name, shape, dt))

        def sem(name):
            return ctx.enter_context(nc.semaphore(name))

        gated = keep("gated", [P, NT, D], F32)
        ident = keep("ident", [P, P], F32)
        ew = keep("ew", [P, E * EC, 2, P], F32R)
        plan = keep("plan", [1, 2 * J + E], I32)
        banks = [ctx.enter_context(nc.psum_tensor(f"bank{i}", [P, 512], F32)) for i in range(8)]
        dispatch(nc, sem, banks, ident, ew, gated, plan, rows_dram, xn_tiles, x_tiles,
                 (w_re0, w_im0, w_re1, w_im1), (b_re0, b_im0, b_re1, b_im1), w_gate, b_gate,
                 w_g, b_g, w1, w2, w3, mix, mix_sums)
        experts(nc, sem, banks, ident, ew, gated, plan, rows_dram, y_dram, x_tiles, xn_tiles,
                y_tiles, out_tiles)


def dispatch(nc, sem, banks, ident, ew, gated, plan, rows_dram, xn_tiles, x_tiles,
             w_proj, b_proj, w_gate, b_gate, w_g, b_g, w1, w2, w3, mix, mix_sums):
    ctx = ExitStack()
    with ctx:
        def sb(name, shape, dt):
            return ctx.enter_context(nc.sbuf_tensor(name, shape, dt))

        PW = UW + E
        ones_bf = sb("ones_bf", [P, P], BF16)
        ident_r = sb("ident_r", [P, P], F32R)
        before = sb("before", [P, P], BF16)
        first_key = sb("first_key", [P, E], F32)
        region = sb("region", [P, E], F32)
        keep_sum = sb("keep_sum", [P, E, GT + 1], F32)
        half_power = sb("half_power", [P, GT], F32)
        steps = sb("steps", [1, J], F32)
        dest = sb("dest", [P, K * GT], F32)
        pad_row = sb("pad_row", [P, ROW], F32)

        proj_hi = sb("proj_hi", [P, UW], F32R)
        proj_lo = sb("proj_lo", [P, UW], F32R)
        route_hi_lo = sb("route_hi_lo", [P, 2 * E], F32R)
        gate_hi = sb("gate_hi", [P, D], F32R)
        gate_lo = sb("gate_lo", [P, D], F32R)
        gbias = sb("gbias", [P, 1], F32)
        mix_hi = sb("mix_hi", [P, SC * 4 * P], F32R)
        mix_lo = sb("mix_lo", [P, SC * 4 * P], F32R)
        h_bias_hi = sb("h_bias_hi", [P, 2, D], F32R)
        h_bias_lo = sb("h_bias_lo", [P, 2, D], F32R)
        g_bias = sb("g_bias", [P, E], F32)

        ew_raw = sb("ew_raw", [P, 2, EW], F32)
        early = gated[:].rearrange("p i d -> p (i d)")
        ones, early = early[:, 0:P], early[:, P:]
        mix_raw, early = early[:, 0:SC * 4 * P], early[:, SC * 4 * P:]
        proj_raw, early = early[:, 0:PW], early[:, PW:]
        gate_raw, early = early[:, 0:D], early[:, D:]
        sums, early = early[0:2, 0:SC * S], early[:, SC * S:]
        pbias, gbias_raw = early[0:2, 0:D], early[:, D:D + 1]
        x_in_sb = sb("x_in_sb", [P, 2, GT, D], F32)
        xn = sb("xn", [P, 2, GT, D], F32)
        stats = sb("stats", [P, GT, 6], F32)
        moments = sb("moments", [P, GT, 2], F32)
        var_eps = sb("var_eps", [P, GT], F32)
        rstd = sb("rstd", [P, GT], F32)
        xt_hi = sb("xt_hi", [P, 2, HT4 * P], F32R)
        xt_lo = sb("xt_lo", [P, 2, HT4 * P], F32R)
        u_hi = sb("u_hi", [P, GT, UW], F32R)
        u_lo = sb("u_lo", [P, GT, UW], F32R)
        h = sb("h", [P, GT, D], F32)
        ht_hi, ht_lo = (t[:, 0:HT4].rearrange("p (h i) d -> p h (i d)", h=2) for t in (u_hi, u_lo))
        tanh_t = gated[:].rearrange("p (n i) d -> p n (i d)", i=HT4)
        rows = sb("rows", [P, 2, K * GT, ROW], F32)
        slot_row = sb("slot_row", [P, 2, K * GT], U32)

        logits = sb("logits", [P, GT, E], F32)
        logits2 = sb("logits2", [P, GT, E], F32)
        key = sb("key", [P, 2, GT, E], F32)
        chosen = sb("chosen", [P, K, GT, E], F32)
        best = sb("best", [P, K, GT], F32)
        best_key = sb("best_key", [P, K, GT], F32)
        gap = sb("gap", [P, GT], F32)
        ratio = sb("ratio", [P, GT], F32)
        denom = sb("denom", [P, GT], F32)
        weight = sb("weight", [P, K, GT], F32)
        mask = sb("mask", [P, E, GT + 1], BF16)
        prefix = sb("prefix", [P, E, GT + 1], BF16)
        position = sb("position", [P, E, GT], F32)
        picked = sb("picked", [P, K, GT, E], F32)

        count = sb("count", [1, E], F32)
        padded = sb("padded", [1, E], I32)
        tiles_i = sb("tiles_i", [1, E], I32)
        tiles_f = sb("tiles_f", [1, E], F32)
        tile_end = sb("tile_end", [1, E], F32)
        jump = sb("jump", [1, E], F32)
        scratch = x_in_sb[0:1].rearrange("p k i d -> p k (i d)")
        passed, jumped = (scratch[:, j, 0:J * E].rearrange("p (j e) -> p j e", e=E) for j in range(2))
        plan_f = scratch[:, 0, J * E:J * E + 2 * J].rearrange("p (a j) -> p a j", a=2)
        plan_g = scratch[:, 1, J * E:J * E + J]

        xt_bank, u_bank, h_bank = banks[0:2], (banks[2], banks[3], banks[7], banks[5]), banks[4:6]
        ht_bank, gate_bank = u_bank, (banks[4], banks[6])
        count_at = xt_bank[0][:, 0:E]
        PAIRS = (2, 3, 0, 1)
        logits_at, pos_at = banks[6][:, 0:2 * GT * E], banks[6][:, 2 * GT * E:3 * GT * E]

        consts_in, proj_in, mix_in = sem("consts_in"), sem("proj_in"), sem("mix_in")
        filled, made = sem("filled"), sem("made")
        split_hi, split_lo = sem("split_hi"), sem("split_lo")
        mix_hi_done, mix_lo_done = sem("mix_hi_done"), sem("mix_lo_done")
        hb_ready, hb_hi_done, hb_lo_done = sem("hb_ready"), sem("hb_hi_done"), sem("hb_lo_done")
        x_first, x_in = sem("x_first"), [sem(f"x_in{k}") for k in range(2)]
        w_in = [sem(f"w_in{k}") for k in range(2)]
        xn_out = [sem(f"xn_out{k}") for k in range(2)]
        groups_sent = sem("groups_sent")
        sent = [sem(f"sent{k}") for k in range(2)]
        stats_done, moments_done, var_done = sem("stats_done"), sem("moments_done"), sem("var_done")
        stats_seen = sem("stats_seen")
        rstd_done, xn_done = sem("rstd_done"), sem("xn_done")
        xt_ready, xt_hi_done, xt_lo_done = sem("xt_ready"), sem("xt_hi_done"), sem("xt_lo_done")
        logits_ready, logits_done = sem("logits_ready"), sem("logits_done")
        u_ready, u_hi_done, u_lo_done = sem("u_ready"), sem("u_hi_done"), sem("u_lo_done")
        h_ready, h_done = sem("h_ready"), sem("h_done")
        ht_ready, ht_hi_done, ht_lo_done = sem("ht_ready"), sem("ht_hi_done"), sem("ht_lo_done")
        gate_ready, tanh_done = sem("gate_ready"), sem("tanh_done")
        tanh_ready, gated_done = sem("tanh_ready"), sem("gated_done")
        route = sem("route")
        gap_done, exp_done, weight_done = sem("gap_done"), sem("exp_done"), sem("weight_done")
        prefix_done, pos_ready = sem("prefix_done"), sem("pos_ready")
        idx_done, dest_done = sem("idx_done"), sem("dest_done")
        row_done = sem("row_done")
        w_hi_done, w_lo_done, w_lo_first = sem("w_hi_done"), sem("w_lo_done"), sem("w_lo_first")
        counts_in, count_ready = sem("counts_in"), sem("count_ready")
        planning, planned = sem("planning"), sem("planned")
        pad_out = sem("pad_out")

        FIRST = 2
        N_CONSTS = 8
        AT_ONCE, BEFORE_NEXT, OF_FIRST = 2, 6, 12
        block = ctx.enter_context(nc.Block())

        @block.sync
        def _(sp):
            def tokens(q):
                if q > 1:
                    sp.wait_ge(xn_done, (q - 1) * GT)
                first = 0 if q else HT4
                sp.dma_start(x_in_sb[:, q % 2, first:], x_tiles[:, q * GT + first:(q + 1) * GT, :]
                             ).then_inc(x_in[q % 2], 16)

            def weights(e):
                j = e % 2
                if e >= FIRST + 2:
                    sp.wait_ge(w_lo_done, e - 1 - FIRST)
                elif e >= 2:
                    sp.wait_ge(w_lo_first, e - 1)
                for m, w in enumerate((w1, w3)):
                    sp.dma_start(ew_raw[:, j, m * HID:(m + 1) * HID], w[e]).then_inc(w_in[j], 16)
                sp.dma_start(ew_raw[:, j, 2 * HID:EW].rearrange("p (c d) -> p c d", c=NC),
                             w2[e].rearrange("(c p) d -> p c d", p=P)).then_inc(w_in[j], 16)

            sp.dma_start(x_in_sb[:, 0, 0:HT4], x_tiles[:, 0:HT4, :]).then_inc(x_first, 16)
            tokens(0)
            sp.dma_start(g_bias[:], b_g.partition_broadcast(P)).then_inc(consts_in, 16)
            tokens(1)
            sp.dma_start(sums, mix_sums).then_inc(consts_in, 16)
            for n, b in enumerate(b_proj):
                sp.dma_start(pbias[n % 2:n % 2 + 1, (n // 2) * DP:(n // 2 + 1) * DP],
                             b.unsqueeze(0)).then_inc(consts_in, 16)
            sp.dma_start(gate_raw, w_gate).then_inc(consts_in, 16)
            sp.dma_start(gbias_raw, b_gate.unsqueeze(1)).then_inc(consts_in, 16)
            weights(0)
            weights(1)
            for q in range(NG):
                sp.wait_ge(xn_done, q * GT + GT)
                sp.dma_start(xn_tiles[:, q * GT:(q + 1) * GT, :], xn[:, q % 2]).then_inc(xn_out[q % 2], 16)
                if q + 2 < NG:
                    tokens(q + 2)
                if q + 1 < NG:
                    weights(2 * q + 2)
                    weights(2 * q + 3)
            sp.wait_ge(filled, 1)
            sp.wait_ge(made, 5)
            sp.dma_start(rows_dram[IDLE:IDLE + P, :], pad_row[:]).then_inc(pad_out, 16)
            sp.wait_ge(planned, 3)
            starts = nc.values_load_multi_w_load_instructions(
                plan[0:1, 2 * J:2 * J + E], engines=[mybir.EngineType.SP], min_val=0, max_val=IDLE - P,
                skip_runtime_bounds_check_because="a count of rows is at most TOK")[1]
            for start in starts:
                sp.dma_start(rows_dram[bass.ds(start, P), :], pad_row[:]).then_inc(pad_out, 16)
            sp.wait_ge(pad_out, 16 * (E + 1))
            for k in range(2):
                sp.wait_ge(xn_out[k], 16 * (NG // 2))

        @block.gpsimd
        def _(pool):
            pool.memset(ones, 1.0).then_inc(filled, 1)
            pool.memset(half_power[:], -0.5).then_inc(filled, 1)
            pool.wait_ge(filled, 2)
            pool.affine_select(out=ident[:], in_=ones, compare_op=ALU.is_equal, fill=0.0, base=0,
                               pattern=[[-1, P]], channel_multiplier=1).then_inc(made, 1)

            def inverse_deviation(q):
                pool.wait_ge(var_done, q + 1)
                if q:
                    pool.wait_ge(xn_done, q * GT)
                pool.tensor_tensor(rstd[:], var_eps[:], half_power[:], ALU.pow).then_inc(rstd_done, 1)

            inverse_deviation(0)
            pool.memset(ones_bf[:], 1.0).then_inc(filled, 1)
            pool.memset(keep_sum[:], 1.0).then_inc(filled, 1)
            pool.memset(mask[:], 0.0).then_inc(filled, 1)
            pool.memset(pad_row[:], 0.0).then_inc(filled, 1)
            pool.iota(first_key[:], [[-1, E]], base=E, channel_multiplier=0,
                      allow_small_or_imprecise_dtypes=True).then_inc(made, 1)
            pool.iota(region[:], [[REG, E]], base=0, channel_multiplier=0,
                      allow_small_or_imprecise_dtypes=True).then_inc(made, 1)
            pool.wait_ge(filled, 6)
            pool.affine_select(out=before[:], in_=ones_bf[:], compare_op=ALU.is_gt, fill=0.0, base=0,
                               pattern=[[1, P]], channel_multiplier=-1).then_inc(made, 1)
            pool.iota(pad_row[:, D:ROW].bitcast(U32), [[0, 1]], base=DUMP, channel_multiplier=1).then_inc(made, 1)
            pool.memset(keep_sum[:, :, 0:1], 0.0).then_inc(made, 1)
            pool.iota(dest[:], [[TOK, K], [1, GT]], base=0, channel_multiplier=NT,
                      allow_small_or_imprecise_dtypes=True).then_inc(made, 1)
            pool.iota(steps[:], [[1, J]], base=0, channel_multiplier=0,
                      allow_small_or_imprecise_dtypes=True).then_inc(made, 1)

            for e in range(FIRST):
                pool.wait_ge(w_hi_done, e + 1)
                pool.tensor_tensor(ew[:, e * EC:(e + 1) * EC, 1], ew_raw[:, e % 2].rearrange("p (c d) -> p c d", c=EC),
                                   ew[:, e * EC:(e + 1) * EC, 0].bitcast(F32), ALU.subtract
                                   ).then_inc(w_lo_first, 1)
            inverse_deviation(1)
            for q in range(NG):
                k = q % 2
                pool.wait_ge(idx_done, q + 1)
                pool.wait_ge(dest_done, q + 1)
                for n in range(K * GT):
                    i, slot = n // K, n % K
                    pool.wait_ge(row_done, q * K * GT + n + 1)
                    at = slot * GT + i
                    pool.indirect_dma_start(
                        out=rows_dram[:, :],
                        out_offset=bass.IndirectOffsetOnAxis(ap=slot_row[:, k, at:at + 1], axis=0),
                        in_=rows[:, k, at, :], in_offset=None).then_inc(sent[k], 16)
                    if n == 2 and 0 < q < NG - 1:
                        pool.wait_ge(sent[1 - k], 16 * K * GT * ((q + 1) // 2))
                        pool.sem_inc(groups_sent, 1)
                    if n == K * GT - 3 and q + 2 < NG:
                        inverse_deviation(q + 2)
            for k in range(2):
                pool.wait_ge(sent[k], 16 * K * GT * (NG // 2))

        @block.scalar
        def _(act):
            for n, w in enumerate(w_proj):
                act.dma_start(proj_raw[:, n * DP:(n + 1) * DP], w).then_inc(proj_in, 16)
            act.dma_start(proj_raw[:, UW:PW], w_g).then_inc(proj_in, 16)
            act.preload_act_table(ACT.Exp)
            act.dma_start(mix_raw, mix).then_inc(mix_in, 16)
            act.wait_ge(proj_in, 16 * 5)
            act.activation(route_hi_lo[:, 0:E], proj_raw[:, UW:PW], ACT.Copy).then_inc(split_hi, 1)
            act.activation(proj_hi[:], proj_raw[:, 0:UW], ACT.Copy).then_inc(split_hi, 1)

            def weights_hi(e):
                act.wait_ge(w_in[e % 2], (e // 2 + 1) * 48)
                act.activation(ew[:, e * EC:(e + 1) * EC, 0], ew_raw[:, e % 2].rearrange("p (c d) -> p c d", c=EC),
                               ACT.Copy).then_inc(w_hi_done, 1)

            def gate_tanh(q):
                for half in range(2):
                    act.wait_ge(gate_ready, q * 2 + half + 1)
                    if q == 0:
                        act.wait_ge(split_lo, 4)
                    act.activation(tanh_t[:, 2 * q + half], gate_bank[half][:], ACT.Tanh, scale=0.5, bias=gbias[:]
                                   ).then_inc(tanh_done, 1)

            def tokens_hi(q):
                for half in range(2):
                    act.wait_ge(xt_ready, q * 2 + half + 1)
                    act.activation(xt_hi[:, half], xt_bank[half][:], ACT.Copy).then_inc(xt_hi_done, 1)

            def h_out(q, tb):
                act.wait_ge(h_ready, q * 2 + tb + 1)
                if q and tb == 0:
                    act.wait_ge(gated_done, q * 2)
                act.activation(h[:].rearrange("p (b t) d -> p t b d", t=2)[:, tb],
                               h_bank[tb][:].rearrange("p (b d) -> p b d", b=GB), ACT.Copy
                               ).then_inc(h_done, 1)

            def h_hi(q):
                for half in range(2):
                    act.wait_ge(ht_ready, q * 2 + half + 1)
                    act.activation(ht_hi[:, half], ht_bank[half][:], ACT.Copy).then_inc(ht_hi_done, 1)

            def projection_hi(q, first, end):
                for n in range(first, end):
                    act.wait_ge(u_ready, q * (GT // 2) + n + 1)
                    p = PAIRS[n]
                    act.activation(u_hi[:, 2 * p:2 * p + 2], u_bank[p][:].rearrange("p (i d) -> p i d", i=2),
                                   ACT.Copy).then_inc(u_hi_done, 1)

            def weighted_rows(q, first, end):
                for n in range(first, end):
                    i, slot = n // K, n % K
                    act.activation(rows[:, q % 2, slot * GT + i, 0:D], xn[:, q % 2, i], ACT.Copy,
                                   scale=weight[:, slot, i:i + 1]).then_inc(row_done, 1)

            def other_tables_hi():
                act.wait_ge(consts_in, 16 * N_CONSTS)
                act.activation(gate_hi[:], gate_raw, ACT.Copy).then_inc(split_hi, 1)
                act.wait_ge(made, 1)
                act.activation(ident_r[:], ident[:], ACT.Copy).then_inc(split_hi, 1)
                act.wait_ge(mix_in, 16)
                act.activation(mix_hi[:], mix_raw, ACT.Copy).then_inc(mix_hi_done, 1)
                act.wait_ge(hb_ready, 1)
                act.activation(h_bias_hi[:].rearrange("p t d -> p (t d)"), h_bank[0][:, 0:2 * D], ACT.Copy
                               ).then_inc(hb_hi_done, 1)

            for q in range(NG):
                tokens_hi(q)
                if q == 0:
                    other_tables_hi()
                else:
                    weighted_rows(q - 1, BEFORE_NEXT if q > 1 else OF_FIRST, K * GT)
                weights_hi(2 * q)
                weights_hi(2 * q + 1)
                if q:
                    h_out(q - 1, 0)
                else:
                    projection_hi(0, 0, 2)
                act.wait_ge(gap_done, q + 1)
                act.activation(ratio[:], gap[:], ACT.Exp).then_inc(exp_done, 1)
                if q:
                    h_out(q - 1, 1)
                else:
                    projection_hi(0, 2, GT // 2)
                act.wait_ge(weight_done, q * 2 + 2)
                if q > 1:
                    act.wait_ge(groups_sent, q - 1)
                weighted_rows(q, 0, AT_ONCE if q else OF_FIRST)
                if q:
                    h_hi(q - 1)
                    projection_hi(q, 0, 2)
                    weighted_rows(q, AT_ONCE, BEFORE_NEXT)
                    gate_tanh(q - 1)
                    projection_hi(q, 2, GT // 2)
            weighted_rows(NG - 1, BEFORE_NEXT, K * GT)
            for tb in range(2):
                h_out(NG - 1, tb)
            h_hi(NG - 1)
            gate_tanh(NG - 1)

        @block.vector
        def _(dve):
            def statistics(q, first, end):
                for i in range(first, end):
                    if i == (0 if q else HT4):
                        dve.wait_ge(x_in[q % 2], q // 2 * 16 + 16)
                    dve.bn_stats(stats[:, i], x_in_sb[:, q % 2, i]).then_inc(stats_done, 1)

            def next_statistics(q, i):
                if q + 1 < NG:
                    statistics(q + 1, i, i + 1)

            def means(q):
                dve.wait_ge(stats_done, q * GT + GT)
                dve.sem_inc(stats_seen, 1)
                for i in range(GT):
                    dve.bn_aggr(moments[:, i], stats[:, i]).then_inc(moments_done, 1)

            def variance(q):
                dve.wait_ge(moments_done, q * GT + GT)
                dve.tensor_scalar(var_eps[:], moments[:, :, 1], EPS, None, ALU.add).then_inc(var_done, 1)

            def projection_lo(q, n):
                dve.wait_ge(u_hi_done, q * (GT // 2) + n + 1)
                p = PAIRS[n]
                dve.tensor_tensor(u_lo[:, 2 * p:2 * p + 2], u_bank[p][:].rearrange("p (i d) -> p i d", i=2),
                                  u_hi[:, 2 * p:2 * p + 2].bitcast(F32), ALU.subtract).then_inc(u_lo_done, 1)

            def weights_lo(e):
                if e < FIRST:
                    return
                dve.wait_ge(w_hi_done, e + 1)
                dve.tensor_tensor(ew[:, e * EC:(e + 1) * EC, 1], ew_raw[:, e % 2].rearrange("p (c d) -> p c d", c=EC),
                                  ew[:, e * EC:(e + 1) * EC, 0].bitcast(F32), ALU.subtract
                                  ).then_inc(w_lo_done, 1)

            def h_lo(q, half):
                dve.wait_ge(ht_hi_done, q * 2 + half + 1)
                dve.tensor_tensor(ht_lo[:, half], ht_bank[half][:], ht_hi[:, half].bitcast(F32),
                                  ALU.subtract).then_inc(ht_lo_done, 1)

            def gated_half(q, half):
                dve.wait_ge(tanh_ready, q * 2 + half + 1)
                dve.scalar_tensor_tensor(
                    out=gated[:, q * GT + half * HT4:q * GT + (half + 1) * HT4, :].rearrange("p i d -> p (i d)"),
                    in0=gate_bank[half][:], scalar=1.0,
                    in1=h[:, half * HT4:(half + 1) * HT4].rearrange("p i d -> p (i d)"),
                    op0=ALU.add, op1=ALU.mult).then_inc(gated_done, 1)

            chained = [0]

            def chain(ins):
                ins.then_inc(route, 1)
                chained[0] += 1

            def chain_wait():
                dve.wait_ge(route, chained[0])

            dve.wait_ge(x_first, 16)
            statistics(0, 0, GT)
            means(0)
            variance(0)
            for q in range(NG):
                k = q % 2
                dve.wait_ge(rstd_done, q + 1)
                if q > 1:
                    dve.wait_ge(xn_out[k], q // 2 * 16)
                    dve.wait_ge(row_done, (q - 1) * K * GT)
                for i in range(GT):
                    dve.tensor_scalar(xn[:, k, i], x_in_sb[:, k, i], moments[:, i, 0:1], rstd[:, i:i + 1],
                                      ALU.subtract, ALU.mult).then_inc(xn_done, 1)
                if q == 0:
                    dve.wait_ge(split_hi, 2)
                    dve.tensor_tensor(route_hi_lo[:, E:2 * E], proj_raw[:, UW:PW],
                                      route_hi_lo[:, 0:E].bitcast(F32), ALU.subtract).then_inc(split_lo, 1)
                    dve.tensor_tensor(proj_lo[:], proj_raw[:, 0:UW], proj_hi[:].bitcast(F32), ALU.subtract
                                      ).then_inc(split_lo, 1)
                else:
                    projection_lo(q - 1, 2)
                    if q > 1:
                        gated_half(q - 2, 1)
                for half in range(2):
                    dve.wait_ge(xt_hi_done, q * 2 + half + 1)
                    dve.tensor_tensor(xt_lo[:, half], xt_bank[half][:], xt_hi[:, half].bitcast(F32),
                                      ALU.subtract).then_inc(xt_lo_done, 1)
                if q:
                    projection_lo(q - 1, 3)
                if q > 1:
                    gated_half(q - 2, 0)
                if q == 0:
                    dve.wait_ge(consts_in, 16 * N_CONSTS)
                    dve.tensor_scalar(gbias[:], gbias_raw, 0.5, None, ALU.mult).then_inc(split_lo, 1)
                    dve.wait_ge(split_hi, 3)
                    dve.tensor_tensor(gate_lo[:], gate_raw, gate_hi[:].bitcast(F32), ALU.subtract
                                      ).then_inc(split_lo, 1)
                    dve.wait_ge(mix_hi_done, 1)
                    dve.tensor_tensor(mix_lo[:], mix_raw, mix_hi[:].bitcast(F32), ALU.subtract
                                      ).then_inc(mix_lo_done, 1)
                    dve.wait_ge(hb_hi_done, 1)
                    dve.tensor_tensor(h_bias_lo[:].rearrange("p t d -> p (t d)"), h_bank[0][:, 0:2 * D],
                                      h_bias_hi[:].rearrange("p t d -> p (t d)").bitcast(F32), ALU.subtract
                                      ).then_inc(hb_lo_done, 1)
                    dve.wait_ge(made, 8)
                dve.wait_ge(logits_ready, q + 1)
                parts = logits_at.rearrange("p (i s e) -> p s i e", s=2, e=E)
                dve.tensor_tensor(logits[:], parts[:, 0], g_bias[:].unsqueeze(1).broadcast_to([P, GT, E]), ALU.add
                                  ).then_inc(logits_done, 1)
                if q + 1 < NG:
                    statistics(q + 1, 0, 1)
                dve.wait_ge(logits_done, q * 2 + 1)
                dve.tensor_tensor(logits[:], parts[:, 1], logits[:], ALU.add).then_inc(logits_done, 1)
                dve.wait_ge(logits_done, q * 2 + 2)
                for s, l in enumerate((logits, logits2)):
                    chain(dve.tensor_reduce(best[:, s], l[:], X, ALU.max))
                    next_statistics(q, 1 + 4 * s)
                    chain_wait()
                    if s:
                        if q:
                            dve.wait_ge(exp_done, q)
                        dve.tensor_tensor(gap[:], best[:, 1], best[:, 0], ALU.subtract).then_inc(gap_done, 1)
                    chain(dve.tensor_tensor(key[:, 0], l[:], best[:, s].unsqueeze(2).broadcast_to([P, GT, E]),
                                            ALU.is_equal))
                    next_statistics(q, 2 + 4 * s)
                    chain_wait()
                    chain(dve.tensor_tensor(key[:, 1], key[:, 0],
                                            first_key[:].unsqueeze(1).broadcast_to([P, GT, E]), ALU.mult))
                    next_statistics(q, 3 + 4 * s)
                    chain_wait()
                    chain(dve.tensor_reduce(best_key[:, s], key[:, 1], X, ALU.max))
                    if s == 0:
                        next_statistics(q, 4)
                    chain_wait()
                    chain(dve.tensor_tensor(chosen[:, s], key[:, 1],
                                            best_key[:, s].unsqueeze(2).broadcast_to([P, GT, E]), ALU.is_equal))
                    chain_wait()
                    if s == 0:
                        chain(dve.scalar_tensor_tensor(out=logits2[:], in0=chosen[:, 0], scalar=LOWEST,
                                                       in1=logits[:], op0=ALU.mult, op1=ALU.add))
                        weights_lo(2 * q)
                        chain_wait()
                if q + 1 < NG:
                    means(q + 1)
                    variance(q + 1)
                dve.wait_ge(exp_done, q + 1)
                chain(dve.tensor_scalar(denom[:], ratio[:], 1.0, None, ALU.add))
                chain(dve.tensor_tensor(mask[:, :, 1:GT + 1], chosen[:, 0].rearrange("p i e -> p e i"),
                                        chosen[:, 1].rearrange("p i e -> p e i"), ALU.add))
                chain_wait()
                if q:
                    dve.wait_ge(row_done, q * K * GT)
                dve.reciprocal(weight[:, 0], denom[:]).then_inc(weight_done, 1)
                dve.tensor_tensor_scan(prefix[:].rearrange("p e i -> p (e i)"),
                                       keep_sum[:].rearrange("p e i -> p (e i)"),
                                       mask[:].rearrange("p e i -> p (e i)"), 0.0, ALU.mult, ALU.add
                                       ).then_inc(prefix_done, 1)
                dve.wait_ge(weight_done, q * 2 + 1)
                dve.tensor_tensor(weight[:, 1], ratio[:], weight[:, 0], ALU.mult).then_inc(weight_done, 1)
                if q > 1:
                    dve.wait_ge(groups_sent, q - 1)
                chain(dve.tensor_copy(rows[:, k, :, D].bitcast(U32), dest[:]))
                dve.wait_ge(pos_ready, q + 1)
                chain(dve.tensor_tensor(position[:], pos_at.rearrange("p (e i) -> p e i", e=E),
                                        region[:].unsqueeze(2).broadcast_to([P, E, GT]), ALU.add))
                chain_wait()
                dve.tensor_scalar(dest[:], dest[:], float(GT), None, ALU.add).then_inc(dest_done, 1)
                chain(dve.tensor_tensor(picked[:], chosen[:],
                                        position[:].rearrange("p e i -> p i e").unsqueeze(1)
                                        .broadcast_to([P, K, GT, E]), ALU.mult))
                dve.tensor_copy(mask[:, :, 0], prefix[:, :, GT]).then_inc(counts_in, 1)
                chain_wait()
                with nc.allow_low_precision(reason="a whole number below 2^24, summed in float32"):
                    dve.tensor_reduce(slot_row[:, k], picked[:].rearrange("p s i e -> p (s i) e"), X, ALU.add
                                      ).then_inc(idx_done, 1)
                weights_lo(2 * q + 1)
                if q:
                    h_lo(q - 1, 0)
                    h_lo(q - 1, 1)
                projection_lo(q, 0)
                projection_lo(q, 1)
                dve.wait_ge(counts_in, q + 1)

            done = [0]

            def then(ins):
                ins.then_inc(planning, 1)
                done[0] += 1
                dve.wait_ge(planning, done[0])

            dve.wait_ge(count_ready, 1)
            then(dve.tensor_copy(count[:], count_at[0:1, :]))
            then(dve.tensor_scalar(padded[:], count[:], float(P - 1), None, ALU.add))
            then(dve.tensor_scalar(tiles_i[:], padded[:], 7, None, ALU.arith_shift_right))
            then(dve.tensor_copy(tiles_f[:], tiles_i[:]))
            then(dve.tensor_tensor_scan(tile_end[:], keep_sum[0:1, 0, 1:E + 1], tiles_f[:], 0.0,
                                        ALU.mult, ALU.add))
            then(dve.tensor_scalar(jump[:], tiles_f[:], float(-P), float(REG), ALU.mult, ALU.add))
            for half in (1, 0):
                gated_half(NG - 2, half)
            for n in (2, 3):
                projection_lo(NG - 1, n)
            then(dve.tensor_tensor(passed, steps[:].unsqueeze(2).broadcast_to([1, J, E]),
                                   tile_end[:].unsqueeze(1).broadcast_to([1, J, E]), ALU.is_ge))
            then(dve.tensor_tensor(jumped, passed, jump[:].unsqueeze(1).broadcast_to([1, J, E]),
                                   ALU.mult))
            then(dve.tensor_reduce(plan_f[:, 0], jumped, X, ALU.add))
            then(dve.tensor_reduce(plan_f[:, 1], passed, X, ALU.add))
            then(dve.scalar_tensor_tensor(out=plan_g, in0=steps[:], scalar=float(P), in1=plan_f[:, 0],
                                          op0=ALU.mult, op1=ALU.add))
            dve.tensor_scalar(plan[:, 0:J], plan_g, float(IDLE), None, ALU.min).then_inc(planned, 1)
            dve.tensor_scalar(plan[:, J:2 * J], plan_f[:, 1], float(E - 1), float(2 * EW), ALU.min, ALU.mult
                              ).then_inc(planned, 1)
            dve.tensor_tensor(plan[:, 2 * J:], count[:], region[0:1, :], ALU.add).then_inc(planned, 1)
            for half in range(2):
                h_lo(NG - 1, half)
            for half in range(2):
                gated_half(NG - 1, half)

        @block.tensor
        def _(pe):
            def product(to, lhs, rhs, first=True, last=True):
                (a_hi, a_lo), (b_hi, b_lo) = lhs, rhs
                pe.matmul(to, a_hi, b_hi, start=first, stop=False, skip_group_check=True)
                pe.matmul(to, a_hi, b_lo, start=False, stop=False, skip_group_check=True)
                return pe.matmul(to, a_lo, b_hi, start=False, stop=last, skip_group_check=True)

            def mixing(q, tb):
                if q:
                    pe.wait_ge(gated_done, q * 2)
                to = h_bank[tb][:].rearrange("p (b d) -> p b d", b=GB)
                for n, b in enumerate((h_bias_hi, h_bias_lo)):
                    pe.matmul(to, ident_r[:], b[:, tb].unsqueeze(1).broadcast_to([P, GB, D]),
                              start=(n == 0), stop=False, skip_group_check=True)
                pe.wait_ge(u_lo_done, (q + 1) * (GT // 2))
                halves = [(0, 1), (1, 0)] if tb else [(0, 0)]
                for i in range(SC):
                    to = h_bank[tb][:].rearrange("p (b s c) -> p b s c", b=GB, s=SC)[:, :, i]
                    terms = [(src, blk, part) for src, blk in halves for part in range(2)]
                    for n, (src, blk, part) in enumerate(terms):
                        at = ((i * 2 + part) * 2 + blk) * P
                        col = (i * 2 + part) * DP
                        u = [t[:].rearrange("p (b t) c -> p t b c", t=2)[:, src, :, col:col + DP]
                             for t in (u_hi, u_lo)]
                        mm = product(to, (mix_hi[:, at:at + P], mix_lo[:, at:at + P]), u,
                                     False, n == len(terms) - 1)
                mm.then_inc(h_ready, 1)

            def tokens_t(q):
                for half in range(2):
                    pe.wait_ge(xn_done, q * GT + (half + 1) * HT4)
                    for i in range(HT4):
                        t = pe.transpose(xt_bank[half][:, i * P:(i + 1) * P], xn[:, q % 2, half * HT4 + i], ident[:])
                    t.then_inc(xt_ready, 1)

            def h_t(q):
                pe.wait_ge(h_done, q * 2 + 2)
                for half in range(2):
                    for i in range(HT4):
                        t = pe.transpose(ht_bank[half][:, i * P:(i + 1) * P], h[:, half * HT4 + i], ident[:])
                    t.then_inc(ht_ready, 1)

            def gate(q):
                if q + 1 < NG:
                    pe.wait_ge(idx_done, q + 2)
                for half in range(2):
                    pe.wait_ge(ht_lo_done, q * 2 + half + 1)
                    product(gate_bank[half][:], (gate_hi[:], gate_lo[:]), (ht_hi[:, half], ht_lo[:, half])
                            ).then_inc(gate_ready, 1)

            def tanh_back(q):
                for half in range(2):
                    pe.wait_ge(tanh_done, q * 2 + half + 1)
                    for i in range(HT4):
                        t = pe.transpose(gate_bank[half][:, i * P:(i + 1) * P], tanh_t[:, 2 * q + half, i * P:(i + 1) * P],
                                         ident[:])
                    t.then_inc(tanh_ready, 1)

            def projection(q, first, end):
                for n in range(first, end):
                    p = PAIRS[n]
                    for i in (2 * p, 2 * p + 1):
                        half, at = i // HT4, (i % HT4) * P
                        mm = product(u_bank[p][:, (i % 2) * UW:(i % 2 + 1) * UW],
                                     (xt_hi[:, half, at:at + P], xt_lo[:, half, at:at + P]),
                                     (proj_hi[:], proj_lo[:]))
                    mm.then_inc(u_ready, 1)

            def bias_of_h():
                pe.wait_ge(consts_in, 16 * N_CONSTS)
                for tb in range(2):
                    for i in range(SC):
                        mm = pe.matmul(h_bank[0][:, tb * D + i * DP:tb * D + (i + 1) * DP],
                                       sums[:, i * S + tb * P:i * S + (tb + 1) * P],
                                       pbias[:, i * DP:(i + 1) * DP], start=True, stop=True)
                mm.then_inc(hb_ready, 1)
                pe.wait_ge(split_lo, 2)

            pe.wait_ge(made, 1)
            for q in range(NG):
                tokens_t(q)
                if q == 0:
                    bias_of_h()
                if q:
                    pe.wait_ge(idx_done, q)
                if q > 1:
                    pe.wait_ge(gated_done, (q - 1) * 2 - 1)
                for i in range(GT):
                    half, at = i // HT4, (i % HT4) * P
                    pe.wait_ge(xt_lo_done, q * 2 + half + 1)
                    to = logits_at[:, 2 * i * E:2 * (i + 1) * E]
                    pe.matmul(to, xt_hi[:, half, at:at + P], route_hi_lo[:], start=True, stop=False,
                              skip_group_check=True)
                    mm = pe.matmul(to[:, 0:E], xt_lo[:, half, at:at + P], route_hi_lo[:, 0:E], start=False,
                                   stop=True, skip_group_check=True)
                mm.then_inc(logits_ready, 1)
                if q:
                    mixing(q - 1, 0)
                    mixing(q - 1, 1)
                else:
                    projection(q, 0, GT // 2)
                pe.wait_ge(prefix_done, q + 1)
                to = pos_at.rearrange("p (e i) -> p e i", e=E)
                pe.matmul(to, before[:], mask[:, :, 1:GT + 1], start=True, stop=False)
                pe.matmul(to, ones_bf[:], prefix[:, :, 0:GT], start=False, stop=True).then_inc(pos_ready, 1)
                if q:
                    h_t(q - 1)
                    projection(q, 0, 2)
                    if q == NG - 1:
                        pe.wait_ge(counts_in, NG)
                        pe.wait_ge(idx_done, NG)
                        pe.matmul(count_at, ones_bf[:], mask[:, :, 0], start=True, stop=True).then_inc(count_ready, 1)
                    gate(q - 1)
                    projection(q, 2, GT // 2)
                    tanh_back(q - 1)
                if q == 0:
                    pe.wait_ge(split_hi, 4)
                    pe.wait_ge(split_lo, 4)
                    pe.wait_ge(mix_lo_done, 1)
                    pe.wait_ge(hb_lo_done, 1)
            mixing(NG - 1, 0)
            mixing(NG - 1, 1)
            h_t(NG - 1)
            gate(NG - 1)
            tanh_back(NG - 1)


def experts(nc, sem, banks, ident, ew, gated, plan, rows_dram, y_dram, x_tiles, xn_tiles,
            y_tiles, out_tiles):
    ctx = ExitStack()
    with ctx:
        def sb(name, shape, dt):
            return ctx.enter_context(nc.sbuf_tensor(name, shape, dt))

        row = sb("row", [P, TURN, ROW], F32)
        xt_hi = sb("row_t_hi", [P, 2, P], F32R)
        xt_lo = sb("row_t_lo", [P, 2, P], F32R)
        silu = sb("silu_a", [P, 2, HID], F32)
        hid = sb("hid", [P, 2, HID], F32)
        ht_hi = sb("hid_t_hi", [P, 2, HID], F32R)
        ht_lo = sb("hid_t_lo", [P, 2, HID], F32R)
        y = sb("y", [P, TURN, D], F32)
        x_all = sb("x_all", [P, NT, D], F32)
        xn_all = sb("xn_all", [P, NT, D], F32)
        pair = sb("pair", [P, K, NT, D], F32)

        a_bank, c_bank, ht_bank = banks[0:2], banks[2:4], banks[4:6]
        xt_bank, y_bank = banks[6], banks[7]

        row_in = [sem(f"row_in{k}") for k in range(TURN)]
        y_out = [sem(f"y_out{k}") for k in range(TURN)]
        xt_ready, xt_hi_done, xt_lo_done = sem("e_xt_ready"), sem("e_xt_hi_done"), sem("e_xt_lo_done")
        a_ready, silu_done = sem("a_ready"), sem("silu_done")
        c_ready, hid_done = sem("c_ready"), sem("hid_done")
        ht_ready, ht_hi_done, ht_lo_done = sem("e_ht_ready"), sem("e_ht_hi_done"), sem("e_ht_lo_done")
        y_ready, y_done, y_seen = sem("y_ready"), sem("y_done"), sem("y_seen")
        tail_in, stored = sem("tail_in"), sem("stored")
        pair_in = [sem(f"pair_in{c}") for c in range(CHUNKS)]
        pair_sum_done, sum_ready, silu2_done = sem("pair_sum_done"), sem("sum_ready"), sem("silu2_done")
        prod_done, res_done = sem("prod_done"), sem("res_done")

        block = ctx.enter_context(nc.Block())

        def tiles(eng, turn, head=1):
            for g in range(head):
                turn(g, TURN)
            with eng.Fori(head, TURNS - 1) as g:
                turn(g, TURN)
            return turn(TURNS - 1, LAST)

        def chunk_of(t, c):
            return t[:, c * CT:(c + 1) * CT, :].rearrange("p i d -> p (i d)")

        def has(j, back):
            return not isinstance(j, int) or 0 <= j - back < J

        def loaded(eng, first, count, most):
            return nc.values_load_multi_w_load_instructions(
                plan[0:1, bass.ds(first, count)], engines=[eng], min_val=0, max_val=most,
                skip_runtime_bounds_check_because="the plan is clamped to this range on the chip")[1]

        def all_results_out(eng):
            for k in range(TURN):
                eng.wait_ge(y_out[k], 16 * (TURNS if k < LAST else TURNS - 1))

        def load_pair(eng, c):
            eng.dma_start(pair[:, :, c * CT:(c + 1) * CT, :], y_tiles[:, :, c * CT:(c + 1) * CT, :]
                          ).then_inc(pair_in[c], 16)

        @block.sync
        def _(sp):
            def turn(g, n):
                starts = loaded(mybir.EngineType.SP, g * TURN, n, IDLE)
                for k in range(n):
                    if not isinstance(g, int) or g:
                        sp.wait_ge(y_out[k], g * 16)
                    sp.dma_start(row[:, k], rows_dram[bass.ds(starts[k], P), :]).then_inc(row_in[k], 16)
                    if k == TURN // 2 and (not isinstance(g, int) or g):
                        part = bass.ds(g * PART - PART, PART)
                        sp.dma_start(x_all[:, part, :], x_tiles[:, part, :]).then_inc(tail_in, 16)
                        sp.dma_start(xn_all[:, part, :], xn_tiles[:, part, :]).then_inc(tail_in, 16)

            tiles(sp, turn)
            all_results_out(sp)
            for c in range(0, CHUNKS, 2):
                load_pair(sp, c)
            for c in range(CHUNKS):
                sp.wait_ge(res_done, c + 1)
                sp.dma_start(out_tiles[:, c * CT:(c + 1) * CT, :], pair[:, 0, c * CT:(c + 1) * CT, :]
                             ).then_inc(stored, 16)
            sp.wait_ge(stored, 16 * CHUNKS)

        @block.gpsimd
        def _(pool):
            def turn(g, n):
                for k in range(n):
                    pool.wait_ge(y_done, g * TURN + k + 1)
                    pool.sem_inc(y_seen, 1)
                    pool.indirect_dma_start(
                        out=y_dram[:, :],
                        out_offset=bass.IndirectOffsetOnAxis(ap=row[:, k, D:ROW].bitcast(U32), axis=0),
                        in_=y[:, k], in_offset=None,
                        bounds_check=DUMP - 1, oob_is_err=False).then_inc(y_out[k], 16)

            tiles(pool, turn, head=0)
            for c in range(1, CHUNKS, 2):
                pool.wait_ge(pair_in[c], 16)
                pool.tensor_tensor(chunk_of(pair[:, 1], c), chunk_of(pair[:, 0], c), chunk_of(pair[:, 1], c), ALU.add
                                   ).then_inc(pair_sum_done, 1)

        @block.scalar
        def _(act):
            act.preload_act_table(ACT.Silu)
            act.sem_inc(a_ready, 1)
            act.sem_inc(ht_ready, 2)

            def row_hi(j, b):
                act.wait_ge(xt_ready, j + 2)
                act.activation(xt_hi[:, b], xt_bank[:, 0:P], ACT.Copy).then_inc(xt_hi_done, 1)

            def hidden_hi(j, b):
                act.wait_ge(ht_ready, j + 2)
                act.activation(ht_hi[:, b], ht_bank[b][:], ACT.Copy).then_inc(ht_hi_done, 1)

            def turn(g, n):
                for k in range(n):
                    j = g * TURN + k
                    if has(j, -1):
                        row_hi(j, (k + 1) % 2)
                    act.wait_ge(a_ready, j + 2)
                    act.activation(silu[:, k % 2], a_bank[k % 2][:], ACT.Silu).then_inc(silu_done, 1)
                    if has(j, 1):
                        hidden_hi(j, (k - 1) % 2)

            row_hi(-1, 0)
            tiles(act, turn)
            hidden_hi(J, (J - 1) % 2)
            all_results_out(act)
            for c in range(1, CHUNKS, 2):
                load_pair(act, c)
            for c in range(CHUNKS):
                act.wait_ge(sum_ready, c + 1)
                act.activation(chunk_of(pair[:, 1], c), banks[c][:], ACT.Silu).then_inc(silu2_done, 1)

        @block.vector
        def _(dve):
            dve.sem_inc(silu_done, 1)
            dve.sem_inc(c_ready, 1)
            dve.sem_inc(ht_hi_done, 2)
            dve.sem_inc(y_ready, 3)

            def row_lo(j, b):
                dve.wait_ge(xt_hi_done, j + 2)
                dve.tensor_tensor(xt_lo[:, b], xt_bank[:, 0:P], xt_hi[:, b].bitcast(F32), ALU.subtract
                                  ).then_inc(xt_lo_done, 1)

            def hidden_lo(j, b):
                dve.wait_ge(ht_hi_done, j + 2)
                dve.tensor_tensor(ht_lo[:, b], ht_bank[b][:], ht_hi[:, b].bitcast(F32), ALU.subtract
                                  ).then_inc(ht_lo_done, 1)

            def result(j, g, k):
                dve.wait_ge(y_ready, j + 2)
                if not isinstance(g, int) or g:
                    dve.wait_ge(y_out[k], g * 16)
                dve.tensor_reduce(y[:, k], y_bank[:, 0:2 * D].rearrange("p (a d) -> p d a", a=2), X, ALU.add
                                  ).then_inc(y_done, 1)

            def turn(g, n):
                for k in range(n):
                    j = g * TURN + k
                    if has(j, -1):
                        row_lo(j, (k + 1) % 2)
                    dve.wait_ge(silu_done, j + 2)
                    dve.wait_ge(c_ready, j + 2)
                    dve.tensor_tensor(hid[:, k % 2], c_bank[k % 2][:], silu[:, k % 2], ALU.mult
                                      ).then_inc(hid_done, 1)
                    if has(j, 2):
                        result(j, g if k >= 2 else g - 1, (k - 2) % TURN)
                    if has(j, 1):
                        hidden_lo(j, (k - 1) % 2)

            row_lo(-1, 0)
            tiles(dve, turn, head=2)
            result(J, TURNS - 1, LAST - 2)
            hidden_lo(J, (J - 1) % 2)
            result(J + 1, TURNS - 1, LAST - 1)

            for c in range(CHUNKS):
                dve.wait_ge(silu2_done, c + 1)
                if c == 0:
                    dve.wait_ge(tail_in, 32 * (TURNS - 1))
                dve.scalar_tensor_tensor(out=chunk_of(pair[:, 0], c), in0=chunk_of(pair[:, 1], c), scalar=0.5,
                                         in1=chunk_of(gated, c), op0=ALU.mult, op1=ALU.mult).then_inc(prod_done, 1)
                dve.wait_ge(prod_done, c + 1)
                dve.tensor_tensor(chunk_of(pair[:, 0], c), chunk_of(pair[:, 0], c), chunk_of(x_all, c), ALU.add
                                  ).then_inc(res_done, 1)

        @block.tensor
        def _(pe):
            pe.sem_inc(hid_done, 1)
            pe.sem_inc(ht_lo_done, 2)

            def transpose_row(g, k):
                pe.wait_ge(row_in[k], g * 16 + 16)
                pe.transpose(xt_bank[:, 0:P], row[:, k, 0:D], ident[:]).then_inc(xt_ready, 1)

            flat = ew[:].rearrange("p c s d -> p (c s d)")

            def chunks(col, c, n=NC):
                w = flat[:, bass.ds(col + 2 * c * P, 2 * n * P)].rearrange("p (c s d) -> p c s d", s=2, d=P)
                return w[:, :, 0], w[:, :, 1]

            def up(b, col):
                for c, bank, ready in ((0, a_bank[b], a_ready), (NC, c_bank[b], c_ready)):
                    hi, lo = chunks(col, c)
                    to = bank[:].rearrange("p (c d) -> p c d", c=NC)
                    pe.matmul(to, xt_hi[:, b], hi, start=True, stop=False)
                    pe.matmul(to, xt_lo[:, b], hi, start=False, stop=False)
                    pe.matmul(to, xt_hi[:, b], lo, start=False, stop=True).then_inc(ready, 1)

            def transpose_hidden(j, b):
                pe.wait_ge(hid_done, j + 1)
                for c in range(NC):
                    t = pe.transpose(ht_bank[b][:, c * P:(c + 1) * P], hid[:, b, c * P:(c + 1) * P], ident[:])
                t.then_inc(ht_ready, 1)

            def down(j, b, col):
                pe.wait_ge(ht_lo_done, j + 1)
                for c in range(NC):
                    w = flat[:, bass.ds(col + 2 * (2 * NC + c) * P, 2 * P)]
                    hi, lo = ht_hi[:, b, c * P:(c + 1) * P], ht_lo[:, b, c * P:(c + 1) * P]
                    pe.matmul(y_bank[:, 0:2 * D], hi, w, start=(c == 0), stop=False, skip_group_check=True)
                    mm = pe.matmul(y_bank[:, 0:D], lo, w[:, 0:D], start=False, stop=(c == NC - 1),
                                   skip_group_check=True)
                mm.then_inc(y_ready, 1)

            def turn(g, n):
                lead = 2 if not isinstance(g, int) or g else 0
                columns = loaded(mybir.EngineType.PE, g * TURN + (J - lead), n + lead, (E - 1) * 2 * EW)
                for k in range(n):
                    j = g * TURN + k
                    pe.wait_ge(xt_lo_done, j + 1)
                    if has(j, -1):
                        transpose_row(g if k < TURN - 1 else g + 1, (k + 1) % TURN)
                    up(k % 2, columns[k + lead])
                    if has(j, 1):
                        transpose_hidden(j, (k - 1) % 2)
                    if has(j, 2):
                        down(j, k % 2, columns[k + lead - 2])
                return columns

            transpose_row(0, 0)
            columns = tiles(pe, turn)
            transpose_hidden(J, (J - 1) % 2)
            down(J, (J - 2) % 2, columns[LAST])
            down(J + 1, (J - 1) % 2, columns[LAST + 1])

            def lay(values, c, first=False, last=False):
                return pe.matmul(banks[c][:], ident[:], chunk_of(values, c), start=first, stop=last,
                                 skip_group_check=True)

            pe.wait_ge(y_done, J)
            pe.wait_ge(tail_in, 32 * (TURNS - 1))
            for c in range(CHUNKS):
                lay(xn_all, c, first=True)
            for c in range(CHUNKS):
                if c % 2:
                    pe.wait_ge(pair_sum_done, c // 2 + 1)
                else:
                    pe.wait_ge(pair_in[c], 16)
                    lay(pair[:, 0], c)
                lay(pair[:, 1], c, last=True).then_inc(sum_ready, 1)


_INS = ["L0_attn_x", "L0_attn_W_re0", "L0_attn_b_re0", "L0_attn_W_im0", "L0_attn_b_im0", "L0_attn_W_re1",
        "L0_attn_b_re1", "L0_attn_W_im1", "L0_attn_b_im1", "L0_attn_W_gate", "L0_attn_b_gate", "L0_ffn_Wg",
        "L0_ffn_bg", "L0_ffn_W1", "L0_ffn_W2", "L0_ffn_W3"]


def kernel(**inputs):
    import concourse.bacc as bacc
    from concourse.bass_utils import run_bass_kernel_spmd

    nc = bacc.Bacc("TRN2", target_bir_lowering=False, num_devices=1)
    blocks, sums = mixing_tables()
    arrays = {f"in_{name}": np.ascontiguousarray(inputs[name]) for name in _INS}
    arrays["mix_blocks"], arrays["mix_sums"] = blocks, sums
    args = [nc.dram_tensor(name, a.shape, mybir.dt.from_np(a.dtype), kind="ExternalInput").ap()
            for name, a in arrays.items()]
    args.append(nc.dram_tensor("out", (B, S, D), F32, kind="ExternalOutput").ap())
    build(nc, *args)
    r = run_bass_kernel_spmd(nc, [arrays], core_ids=[0])
    return r.results[0]["out"]
```
